# Optimizing a Trainium2 kernel written in Bass

```python
import numpy as np
import jax
import jax.numpy as jnp

def _softmax(x, axis=-1):
    return jax.nn.softmax(x, axis=axis)

def _gelu(x):
    return jax.nn.gelu(x, approximate=True)

def _silu(x):
    return jax.nn.silu(x)

def _sigmoid(x):
    return jax.nn.sigmoid(x)

def _layernorm(x, axis=-1, eps=1e-05):
    m = jnp.mean(x, axis=axis, keepdims=True)
    v = jnp.var(x, axis=axis, keepdims=True)
    return (x - m) / jnp.sqrt(v + eps)

def _scatter_add(tgt, idx, src, axis=0):
    return tgt.at[idx].add(src)

def _segment_sum(src, seg, n):
    return jax.ops.segment_sum(src, seg, n)
kernel_name = 'mk_dlrm_tower_d1_rec_r8_866697'

def setup_inputs(seed: int=0):
    np.random.seed(seed)
    _w = jnp.asarray

    def _rec_inputs():
        import jax
        import jax.numpy as jnp
        _tk = jax.random.key(seed)
        dense_ctx = jax.random.normal(jax.random.fold_in(_tk, 190), (1024, 16), jnp.float32)
        ids = jnp.stack([jax.random.randint(jax.random.fold_in(_tk, 200 + f), (1024,), 0, v, jnp.int32) for f, v in enumerate([1250, 1000, 125000, 12500, 12500, 125000, 1250, 12500, 125000, 12500, 1250, 1000, 1000, 12500, 1000, 1000, 1250, 12500, 1000, 12500, 1250, 1000, 12500, 1250, 1000, 1000, 1250, 1250, 1250, 1000, 1000, 1000])], axis=1)
        tbl_0 = 0.05 * jax.random.normal(jax.random.fold_in(_tk, 500 + 0), (1250, 64), jnp.float32)
        tbl_1 = 0.05 * jax.random.normal(jax.random.fold_in(_tk, 500 + 1), (1000, 64), jnp.float32)
        tbl_2 = 0.05 * jax.random.normal(jax.random.fold_in(_tk, 500 + 2), (125000, 64), jnp.float32)
        tbl_3 = 0.05 * jax.random.normal(jax.random.fold_in(_tk, 500 + 3), (12500, 64), jnp.float32)
        tbl_4 = 0.05 * jax.random.normal(jax.random.fold_in(_tk, 500 + 4), (12500, 64), jnp.float32)
        tbl_5 = 0.05 * jax.random.normal(jax.random.fold_in(_tk, 500 + 5), (125000, 64), jnp.float32)
        tbl_6 = 0.05 * jax.random.normal(jax.random.fold_in(_tk, 500 + 6), (1250, 64), jnp.float32)
        tbl_7 = 0.05 * jax.random.normal(jax.random.fold_in(_tk, 500 + 7), (12500, 64), jnp.float32)
        tbl_8 = 0.05 * jax.random.normal(jax.random.fold_in(_tk, 500 + 8), (125000, 64), jnp.float32)
        tbl_9 = 0.05 * jax.random.normal(jax.random.fold_in(_tk, 500 + 9), (12500, 64), jnp.float32)
        tbl_10 = 0.05 * jax.random.normal(jax.random.fold_in(_tk, 500 + 10), (1250, 64), jnp.float32)
        tbl_11 = 0.05 * jax.random.normal(jax.random.fold_in(_tk, 500 + 11), (1000, 64), jnp.float32)
        tbl_12 = 0.05 * jax.random.normal(jax.random.fold_in(_tk, 500 + 12), (1000, 64), jnp.float32)
        tbl_13 = 0.05 * jax.random.normal(jax.random.fold_in(_tk, 500 + 13), (12500, 64), jnp.float32)
        tbl_14 = 0.05 * jax.random.normal(jax.random.fold_in(_tk, 500 + 14), (1000, 64), jnp.float32)
        tbl_15 = 0.05 * jax.random.normal(jax.random.fold_in(_tk, 500 + 15), (1000, 64), jnp.float32)
        tbl_16 = 0.05 * jax.random.normal(jax.random.fold_in(_tk, 500 + 16), (1250, 64), jnp.float32)
        tbl_17 = 0.05 * jax.random.normal(jax.random.fold_in(_tk, 500 + 17), (12500, 64), jnp.float32)
        tbl_18 = 0.05 * jax.random.normal(jax.random.fold_in(_tk, 500 + 18), (1000, 64), jnp.float32)
        tbl_19 = 0.05 * jax.random.normal(jax.random.fold_in(_tk, 500 + 19), (12500, 64), jnp.float32)
        tbl_20 = 0.05 * jax.random.normal(jax.random.fold_in(_tk, 500 + 20), (1250, 64), jnp.float32)
        tbl_21 = 0.05 * jax.random.normal(jax.random.fold_in(_tk, 500 + 21), (1000, 64), jnp.float32)
        tbl_22 = 0.05 * jax.random.normal(jax.random.fold_in(_tk, 500 + 22), (12500, 64), jnp.float32)
        tbl_23 = 0.05 * jax.random.normal(jax.random.fold_in(_tk, 500 + 23), (1250, 64), jnp.float32)
        tbl_24 = 0.05 * jax.random.normal(jax.random.fold_in(_tk, 500 + 24), (1000, 64), jnp.float32)
        tbl_25 = 0.05 * jax.random.normal(jax.random.fold_in(_tk, 500 + 25), (1000, 64), jnp.float32)
        tbl_26 = 0.05 * jax.random.normal(jax.random.fold_in(_tk, 500 + 26), (1250, 64), jnp.float32)
        tbl_27 = 0.05 * jax.random.normal(jax.random.fold_in(_tk, 500 + 27), (1250, 64), jnp.float32)
        tbl_28 = 0.05 * jax.random.normal(jax.random.fold_in(_tk, 500 + 28), (1250, 64), jnp.float32)
        tbl_29 = 0.05 * jax.random.normal(jax.random.fold_in(_tk, 500 + 29), (1000, 64), jnp.float32)
        tbl_30 = 0.05 * jax.random.normal(jax.random.fold_in(_tk, 500 + 30), (1000, 64), jnp.float32)
        tbl_31 = 0.05 * jax.random.normal(jax.random.fold_in(_tk, 500 + 31), (1000, 64), jnp.float32)
        _rk = jax.random.fold_in(_tk, 7)
        W_top1 = 0.0693375 * jax.random.normal(jax.random.fold_in(_tk, 801), (208, 512), jnp.float32)
        W_top2 = 0.0441942 * jax.random.normal(jax.random.fold_in(_tk, 802), (512, 256), jnp.float32)
        W_top3 = 0.0625 * jax.random.normal(jax.random.fold_in(_tk, 803), (256, 1), jnp.float32)
        b_top1 = jnp.zeros((512,), jnp.float32)
        b_top2 = jnp.zeros((256,), jnp.float32)
        return (dense_ctx, ids, tbl_0, tbl_1, tbl_2, tbl_3, tbl_4, tbl_5, tbl_6, tbl_7, tbl_8, tbl_9, tbl_10, tbl_11, tbl_12, tbl_13, tbl_14, tbl_15, tbl_16, tbl_17, tbl_18, tbl_19, tbl_20, tbl_21, tbl_22, tbl_23, tbl_24, tbl_25, tbl_26, tbl_27, tbl_28, tbl_29, tbl_30, tbl_31, W_top1, b_top1, W_top2, b_top2, W_top3)
    dense_ctx, ids, tbl_0, tbl_1, tbl_2, tbl_3, tbl_4, tbl_5, tbl_6, tbl_7, tbl_8, tbl_9, tbl_10, tbl_11, tbl_12, tbl_13, tbl_14, tbl_15, tbl_16, tbl_17, tbl_18, tbl_19, tbl_20, tbl_21, tbl_22, tbl_23, tbl_24, tbl_25, tbl_26, tbl_27, tbl_28, tbl_29, tbl_30, tbl_31, W_top1, b_top1, W_top2, b_top2, W_top3 = _rec_inputs()

    def _L0_rec_setup():
        import jax, jax.numpy as jnp
        import numpy as np
        F0 = 32
        D = 64
        B = 256

        def _cin_layer(h, h0, W, b):
            Hn = h.shape[1]
            Mn = h0.shape[1]
            Wr = W.reshape(W.shape[0], Hn, Mn)
            x = jnp.einsum('bhd,bmd,ohm->bod', h, h0, Wr) + b[None, :, None]
            return jax.nn.relu(x)
        key = jax.random.key(seed)
        k1, k2, k3 = jax.random.split(key, 3)
        inputs = jax.random.normal(k1, (B, F0, D), dtype=jnp.float32)
        W1 = jax.random.normal(k2, (128, F0 * F0), dtype=jnp.float32) * (1.0 / np.sqrt(F0 * F0))
        b1 = jnp.zeros((128,), dtype=jnp.float32)
        W2 = jax.random.normal(k3, (128, 64 * F0), dtype=jnp.float32) * (1.0 / np.sqrt(64 * F0))
        b2 = jnp.zeros((128,), dtype=jnp.float32)
        return {'inputs': inputs, 'W1': W1, 'b1': b1, 'W2': W2, 'b2': b2}
    _L0_rec_all = _L0_rec_setup()
    _L0_rec_in = {k: v for k, v in _L0_rec_all.items() if k in ('W1', 'b1', 'W2', 'b2')}
    del _L0_rec_all
    return {'dense_ctx': dense_ctx, 'ids': ids, 'tbl_0': tbl_0, 'tbl_1': tbl_1, 'tbl_2': tbl_2, 'tbl_3': tbl_3, 'tbl_4': tbl_4, 'tbl_5': tbl_5, 'tbl_6': tbl_6, 'tbl_7': tbl_7, 'tbl_8': tbl_8, 'tbl_9': tbl_9, 'tbl_10': tbl_10, 'tbl_11': tbl_11, 'tbl_12': tbl_12, 'tbl_13': tbl_13, 'tbl_14': tbl_14, 'tbl_15': tbl_15, 'tbl_16': tbl_16, 'tbl_17': tbl_17, 'tbl_18': tbl_18, 'tbl_19': tbl_19, 'tbl_20': tbl_20, 'tbl_21': tbl_21, 'tbl_22': tbl_22, 'tbl_23': tbl_23, 'tbl_24': tbl_24, 'tbl_25': tbl_25, 'tbl_26': tbl_26, 'tbl_27': tbl_27, 'tbl_28': tbl_28, 'tbl_29': tbl_29, 'tbl_30': tbl_30, 'tbl_31': tbl_31, 'W_top1': W_top1, 'b_top1': b_top1, 'W_top2': W_top2, 'b_top2': b_top2, 'W_top3': W_top3, 'L0_rec_W1': _L0_rec_in['W1'], 'L0_rec_b1': _L0_rec_in['b1'], 'L0_rec_W2': _L0_rec_in['W2'], 'L0_rec_b2': _L0_rec_in['b2']}

def reference(dense_ctx, ids, tbl_0, tbl_1, tbl_2, tbl_3, tbl_4, tbl_5, tbl_6, tbl_7, tbl_8, tbl_9, tbl_10, tbl_11, tbl_12, tbl_13, tbl_14, tbl_15, tbl_16, tbl_17, tbl_18, tbl_19, tbl_20, tbl_21, tbl_22, tbl_23, tbl_24, tbl_25, tbl_26, tbl_27, tbl_28, tbl_29, tbl_30, tbl_31, W_top1, b_top1, W_top2, b_top2, W_top3, L0_rec_W1, L0_rec_b1, L0_rec_W2, L0_rec_b2):
    import jax
    import jax.numpy as jnp

    def _L0_rec_ref(inputs, W1, b1, W2, b2):
        import jax, jax.numpy as jnp
        import numpy as np
        F0 = 32
        D = 64
        B = 256

        def _cin_layer(h, h0, W, b):
            Hn = h.shape[1]
            Mn = h0.shape[1]
            Wr = W.reshape(W.shape[0], Hn, Mn)
            x = jnp.einsum('bhd,bmd,ohm->bod', h, h0, Wr) + b[None, :, None]
            return jax.nn.relu(x)
        h0 = inputs
        x1 = _cin_layer(h0, h0, W1, b1)
        next_hidden = x1[:, :64]
        direct1 = x1[:, 64:]
        direct2 = _cin_layer(next_hidden, h0, W2, b2)
        result = jnp.concatenate([direct1, direct2], axis=1)
        return jnp.sum(result, axis=-1)
    e = jnp.stack([tbl_0[ids[:, 0]], tbl_1[ids[:, 1]], tbl_2[ids[:, 2]], tbl_3[ids[:, 3]], tbl_4[ids[:, 4]], tbl_5[ids[:, 5]], tbl_6[ids[:, 6]], tbl_7[ids[:, 7]], tbl_8[ids[:, 8]], tbl_9[ids[:, 9]], tbl_10[ids[:, 10]], tbl_11[ids[:, 11]], tbl_12[ids[:, 12]], tbl_13[ids[:, 13]], tbl_14[ids[:, 14]], tbl_15[ids[:, 15]], tbl_16[ids[:, 16]], tbl_17[ids[:, 17]], tbl_18[ids[:, 18]], tbl_19[ids[:, 19]], tbl_20[ids[:, 20]], tbl_21[ids[:, 21]], tbl_22[ids[:, 22]], tbl_23[ids[:, 23]], tbl_24[ids[:, 24]], tbl_25[ids[:, 25]], tbl_26[ids[:, 26]], tbl_27[ids[:, 27]], tbl_28[ids[:, 28]], tbl_29[ids[:, 29]], tbl_30[ids[:, 30]], tbl_31[ids[:, 31]]], axis=1)
    z = _L0_rec_ref(e, L0_rec_W1, L0_rec_b1, L0_rec_W2, L0_rec_b2)
    z = z.reshape(z.shape[0], -1)
    h = jnp.concatenate([z, dense_ctx], axis=1)
    h = jnp.maximum(h @ W_top1 + b_top1, 0.0)
    h = jnp.maximum(h @ W_top2 + b_top2, 0.0)
    y = h @ W_top3
    return y

_drawn_inputs = setup_inputs


def setup_inputs(seed=0):
    import zlib

    import numpy as np

    out = dict(_drawn_inputs(seed))
    spreads = {'b_top1': (0.0, 2.0),
     'b_top2': (0.0, 2.0),
     'L0_rec_b1': (0.0, 0.332),
     'L0_rec_b2': (0.0, 0.709)}
    factors = {'tbl_0': 8.0,
     'tbl_1': 8.0,
     'tbl_2': 8.0,
     'tbl_3': 8.0,
     'tbl_4': 8.0,
     'tbl_5': 8.0,
     'tbl_6': 8.0,
     'tbl_7': 8.0,
     'tbl_8': 8.0,
     'tbl_9': 8.0,
     'tbl_10': 8.0,
     'tbl_11': 8.0,
     'tbl_12': 8.0,
     'tbl_13': 8.0,
     'tbl_14': 8.0,
     'tbl_15': 8.0,
     'tbl_16': 8.0,
     'tbl_17': 8.0,
     'tbl_18': 8.0,
     'tbl_19': 8.0,
     'tbl_20': 8.0,
     'tbl_21': 8.0,
     'tbl_22': 8.0,
     'tbl_23': 8.0,
     'tbl_24': 8.0,
     'tbl_25': 8.0,
     'tbl_26': 8.0,
     'tbl_27': 8.0,
     'tbl_28': 8.0,
     'tbl_29': 8.0,
     'tbl_30': 8.0,
     'tbl_31': 8.0,
     'L0_rec_W1': 8.0,
     'L0_rec_W2': 8.0,
     'dense_ctx': 8.0}
    for name, (base, spread) in spreads.items():
        noise = np.random.default_rng([zlib.crc32(name.encode()), seed]).standard_normal(out[name].shape)
        drawn = base * np.exp(spread * noise) if base else spread * noise
        out[name] = jnp.asarray(drawn.astype(out[name].dtype))
    for name, factor in factors.items():
        out[name] = (out[name] * factor).astype(out[name].dtype)
    return out
```

```python
import numpy as np
import concourse.bass as bass
from concourse import mybir
from contextlib import ExitStack

B, F0, D = 1024, 32, 64
O = 128
HID = 64
DENSE, TOP1, TOP2 = 16, 512, 256
ROWS = [1250, 1000, 125000, 12500, 12500, 125000, 1250, 12500, 125000, 12500, 1250, 1000, 1000, 12500, 1000, 1000,
        1250, 12500, 1000, 12500, 1250, 1000, 12500, 1250, 1000, 1000, 1250, 1250, 1250, 1000, 1000, 1000]

P = 128
N = 1024
HALF = 512
EX = N // D
CH = B // EX
JG = EX // 2
GROUPS = CH // 2
REPS = P // F0
LOOPS = CH // 2 - 1
PAIRS1, PAIRS2 = 2, 8
STORES = 4
ROT = 6

SPLIT = (1, 3, 5)
PE_ORDER = (0, 2, 1, 4, 3, 6, 5, 7)
NS = len(SPLIT)
PE_DONE = {t: PE_ORDER.index(t) + 1 for t in range(PAIRS2)}


def build(nc, table, ids, base, dense, w1a, w1b, w1c, w2, b1, b2, wt1a, wt1b, bt1, wt2, bt2, wt3, y):
    F32, F32R, I32 = mybir.dt.float32, mybir.dt.float32r, mybir.dt.int32
    ALU, ACT, AX = mybir.AluOpType, mybir.ActivationFunctionType, mybir.AxisListType

    ctx = ExitStack()
    with ctx:
        def sb(name, shape, dt=F32):
            return ctx.enter_context(nc.sbuf_tensor(name, shape, dt))

        def sem(name):
            return ctx.enter_context(nc.semaphore(name))

        scratch = nc.dram_tensor("fields_twice", [CH, 2 * F0, N], F32, kind="Internal").ap()

        ids_sb = sb("ids_sb", [P, B // REPS + JG], I32)
        base_sb = sb("base_sb", [P, B // REPS + JG], I32)
        row_no = sb("row_no", [P, 2, JG], I32)
        gathered = sb("gathered", [P, 2, JG * D])
        fields = sb("fields", [P, 2, N])
        rot_lo = sb("rot_lo", [P, 2, 4, N])
        rot_hi = sb("rot_hi", [P, 4, N])
        x1 = sb("x1", [P, N])
        x1_arr = sb("x1_arr", [P, 2, 2, N])
        z1 = sb("z1", [P, 2, 2, N])
        z5 = sb("z5", [3 * F0, N])
        z5_parts = sb("z5_parts", [3 * F0, N], F32R)
        z2 = sb("z2", [P, 4, 2, N])
        z2_high = sb("z2_high", [P, 2, N], F32R)
        z2_low = sb("z2_low", [P, 2, N], F32R)
        x2 = sb("x2", [P, N])
        w1_sb = sb("w1_sb", [P, 4, O])
        w1b_sb = sb("w1b_sb", [P, 4, O])
        w5_sb = sb("w5_sb", [3 * F0, O])
        w5_parts = sb("w5_parts", [3 * F0, O], F32R)
        w2_sb = sb("w2_sb", [P, 2 * PAIRS2, O])
        w2_high = sb("w2_high", [P, 2 * NS, O], F32R)
        w2_low = sb("w2_low", [P, 2 * NS, O], F32R)
        b1_sb = sb("b1_sb", [P, 1])
        b2_sb = sb("b2_sb", [P, 1])
        feat_a = sb("feat_a", [P, B])
        feat_b = sb("feat_b", [P, B])
        wt1a_sb = sb("wt1a_sb", [P, TOP1])
        wt1b_sb = sb("wt1b_sb", [P, TOP1])
        wt2_sb = sb("wt2_sb", [P, 4, TOP2])
        wt3_sb = sb("wt3_sb", [P, 2])
        bt1_sb = sb("bt1_sb", [P, 4])
        bt2_sb = sb("bt2_sb", [P, 2])
        h1 = z2[:, 0:2, :, :].rearrange("p a b n -> p (a b) n")
        h2 = z2[:, 2, :, :]
        y_sb = x1[0:1, :]

        ps1 = ctx.enter_context(nc.psum_tensor("ps1", [P, 2, HALF], F32))
        ps2 = ctx.enter_context(nc.psum_tensor("ps2", [P, 2, HALF], F32))
        pst = ctx.enter_context(nc.psum_tensor("pst", [P, 4, HALF], F32))

        ids_here = sem("ids_here")
        w1_here, w2_here, top_here = sem("w1_here"), sem("w2_here"), sem("top_here")
        w1_ready, w5_high, w5_ready = sem("w1_ready"), sem("w5_high"), sem("w5_ready")
        w2h_ready, w2_ready = sem("w2h_ready"), sem("w2_ready")
        feat_zero = sem("feat_zero")
        row_ready = sem("row_ready")
        rows_here = [sem(f"rows_here{s}") for s in range(2)]
        stored = sem("stored")
        fields_here = sem("fields_here")
        rot_lo_here = [sem(f"rot_lo_here{s}") for s in range(2)]
        rot_hi_here = sem("rot_hi_here")
        z1_ready, z5_ready, z5h_ready, z5_split = sem("z1_ready"), sem("z5_ready"), sem("z5h_ready"), sem("z5_split")
        z2_ready, high_ready, low_ready = sem("z2_ready"), sem("high_ready"), sem("low_ready")
        mm1_done, mm2_done = sem("mm1_done"), sem("mm2_done")
        x1_ready, x2_ready = sem("x1_ready"), sem("x2_ready")
        x1_arr_here = [sem(f"x1_arr_here{s}") for s in range(2)]
        sum1_done, sum2_done = sem("sum1_done"), sem("sum2_done")
        top_mm, h1_ready, h2_ready, y_ready, y_stored = (sem("top_mm"), sem("h1_ready"), sem("h2_ready"),
                                                         sem("y_ready"), sem("y_stored"))

        block = ctx.enter_context(nc.Block())

        def window(i, k, first, count):
            return bass.AP(tensor=scratch.tensor, offset=(2 * i + k) * (2 * F0 * N) + first * N,
                           ap=[[N, count], [N, F0], [1, N]])

        def same(i, k, first):
            return bass.AP(tensor=scratch.tensor, offset=(2 * i + k) * (2 * F0 * N) + first * N,
                           ap=[[0, REPS], [N, F0], [1, N]])

        @block.sync
        def _(sp):
            sp.dma_start(ids_sb[:], ids).then_inc(ids_here, 16)
            sp.dma_start(base_sb[:], base).then_inc(ids_here, 16)
            sp.dma_start(w1_sb[:], w1a).then_inc(w1_here, 16)
            sp.dma_start(w1b_sb[:], w1b).then_inc(w1_here, 16)
            sp.dma_start(w5_sb[:], w1c).then_inc(w1_here, 16)
            sp.dma_start(b1_sb[:], b1).then_inc(w1_here, 16)
            sp.dma_start(b2_sb[:], b2).then_inc(w1_here, 16)
            sp.dma_start(w2_sb[:], w2).then_inc(w2_here, 16)

            def load_fields(i, k):
                sp.dma_start(fields[:, 0, :], same(i, k, 0)).then_inc(fields_here, 16)
                sp.dma_start(fields[:, 1, :], same(i, k, F0 // 2)).then_inc(fields_here, 16)

            def load_rot_lo(i, k):
                for t in range(4):
                    sp.dma_start(rot_lo[:, k % 2, t, :], window(i, k, 4 * t, REPS)).then_inc(rot_lo_here[k % 2], 16)

            def load_rot_hi(i, k):
                for t in range(4):
                    sp.dma_start(rot_hi[:, t, :], window(i, k, 4 * t + 16, REPS)).then_inc(rot_hi_here, 16)

            sp.wait_ge(stored, 16 * STORES)
            load_fields(0, 0)
            load_rot_lo(0, 0)
            load_rot_hi(0, 0)
            load_rot_lo(0, 1)
            sp.wait_ge(z1_ready, PAIRS1)
            sp.wait_ge(z5_ready, 1)
            load_fields(0, 1)
            sp.wait_ge(feat_zero, 1)
            sp.dma_start(feat_b[0:DENSE, :], dense).then_inc(top_here, 16)
            for dst, src in ((wt1a_sb, wt1a), (wt1b_sb, wt1b), (wt2_sb, wt2), (wt3_sb, wt3), (bt1_sb, bt1),
                             (bt2_sb, bt2)):
                sp.dma_start(dst[:], src).then_inc(top_here, 16)

            def phase(i, k, last=False):
                if not last:
                    if k == 0:
                        sp.wait_ge(stored, 16 * STORES * (i + 2))
                    sp.wait_ge(z1_ready, PAIRS1 * (2 * i + k + 2))
                    sp.wait_ge(z5_ready, 2 * i + k + 2)
                    load_fields(i, k + 2)
                    sp.wait_ge(z2_ready, PAIRS2 * (2 * i + k) + 4)
                    load_rot_lo(i, k + 2)
                sp.wait_ge(z2_ready, PAIRS2 * (2 * i + k + 1))
                load_rot_hi(i, k + 1)

            with sp.Fori(0, LOOPS) as i:
                phase(i, 0)
                phase(i, 1)
            phase(LOOPS, 0, last=True)
            sp.wait_ge(y_ready, 2)
            sp.dma_start(y, y_sb).then_inc(y_stored, 16)
            sp.wait_ge(y_stored, 16)

        @block.gpsimd
        def _(pool):
            pool.memset(feat_b[:], 0.0).then_inc(feat_zero, 1)
            pool.wait_ge(ids_here, 32)

            def row_numbers(i, s):
                cols = bass.ds((2 * i + s) * JG, JG)
                pool.tensor_tensor(row_no[:, s % 2, :], ids_sb[:, cols], base_sb[:, cols],
                                   op=ALU.add).then_inc(row_ready, 1)

            def group(i, s, first=False):
                for j in range(JG):
                    pool.indirect_dma_start(gathered[:, s, j * D:(j + 1) * D], None, table,
                                            bass.IndirectOffsetOnAxis(ap=row_no[:, s, j:j + 1], axis=0)
                                            ).then_inc(rows_here[s], 16)
                row_numbers(i, s + 1)
                pool.wait_ge(row_ready, 2 * i + s + 2)
                pool.wait_ge(rows_here[s], 16 * JG * (i + 1))
                if not first:
                    pool.wait_ge(stored, 16 * STORES * (2 * i + s))
                for qp in range(2):
                    for copy in range(2):
                        dst = bass.AP(tensor=scratch.tensor,
                                      offset=(2 * i + s) * (4 * F0 * N) + qp * (2 * F0 * N) + copy * (F0 * N),
                                      ap=[[JG * D, 2], [N, F0], [1, JG * D]])
                        pool.dma_start(dst, gathered[64 * qp:64 * qp + 64, s, :]).then_inc(stored, 16)

            row_numbers(0, 0)
            pool.wait_ge(row_ready, 1)
            group(0, 0, first=True)
            group(0, 1)
            with pool.Fori(1, GROUPS // 2) as i:
                group(i, 0)
                group(i, 1)

        @block.vector
        def _(dve):
            dve.wait_ge(w1_here, 80)
            dve.tensor_tensor(w1_sb[:], w1_sb[:], w1b_sb[:], op=ALU.add).then_inc(w1_ready, 1)
            dve.tensor_copy(w5_parts[:], w5_sb[:]).then_inc(w5_high, 1)
            dve.wait_ge(w5_high, 1)
            dve.tensor_tensor(w5_parts[64:96, :], w5_sb[64:96, :], w5_parts[64:96, :].bitcast(F32),
                              op=ALU.subtract).then_inc(w5_ready, 1)
            dve.wait_ge(w2_here, 16)
            for n, t in enumerate(SPLIT):
                dve.tensor_copy(w2_high[:, 2 * n:2 * n + 2, :], w2_sb[:, 2 * t:2 * t + 2, :]).then_inc(w2h_ready, 1)
            for n, t in enumerate(SPLIT):
                dve.wait_ge(w2h_ready, n + 1)
                dve.tensor_tensor(w2_low[:, 2 * n:2 * n + 2, :], w2_sb[:, 2 * t:2 * t + 2, :],
                                  w2_high[:, 2 * n:2 * n + 2, :].bitcast(F32), op=ALU.subtract).then_inc(w2_ready, 1)

            def products1(i, k, first=False):
                dve.wait_ge(fields_here, 32 * (2 * i + k + 1))
                if not first:
                    dve.wait_ge(z5_split, 2 * i + k)
                dve.tensor_tensor(z5[:], fields[0:96, 0, :], fields[0:96, 1, :], op=ALU.mult).then_inc(z5_ready, 1)
                dve.wait_ge(rot_lo_here[k % 2], 64 * (i + k // 2 + 1))
                for j in range(PAIRS1):
                    if not first:
                        dve.wait_ge(mm1_done, 3 * (2 * i + k - 1) + j + 1)
                    dve.tensor_tensor(z1[:, j, :, :], fields[:, 0:1, :].to_broadcast([P, 2, N]),
                                      rot_lo[:, k % 2, 2 * j:2 * j + 2, :], op=ALU.mult).then_inc(z1_ready, 1)
                dve.wait_ge(z5h_ready, 2 * i + k + 1)
                dve.tensor_tensor(z5_parts[32:64, :], z5[32:64, :], z5_parts[32:64, :].bitcast(F32),
                                  op=ALU.subtract).then_inc(z5_split, 1)

            def low(i, k, n):
                dve.wait_ge(high_ready, NS * (2 * i + k) + n + 1)
                dve.tensor_tensor(z2_low[:], z2[:, SPLIT[n] % 4, :, :], z2_high[:].bitcast(F32),
                                  op=ALU.subtract).then_inc(low_ready, 1)

            def sum1(i, k):
                dve.wait_ge(x1_ready, 2 * i + k + 1)
                dve.tensor_reduce(feat_b[64:128, bass.ds((2 * i + k) * EX, EX)],
                                  x1[64:128, :].rearrange("p (e d) -> p e d", d=D), axis=AX.X,
                                  op=ALU.add).then_inc(sum1_done, 1)

            def sum2(i, k):
                dve.wait_ge(x2_ready, 2 * i + k + 1)
                dve.tensor_reduce(feat_a[:, bass.ds((2 * i + k) * EX, EX)],
                                  x2[:].rearrange("p (e d) -> p e d", d=D), axis=AX.X,
                                  op=ALU.add).then_inc(sum2_done, 1)

            def products2(i, k, first=False, last=False):
                dve.wait_ge(x1_arr_here[k], 16 * ROT * (i + 1))
                for t in range(PAIRS2):
                    if t == 4:
                        dve.wait_ge(rot_hi_here, 64 * (2 * i + k + 1))
                    before, was = (0, t - 4) if t >= 4 else (1, t + 4)
                    if not (first and before):
                        if was in SPLIT:
                            dve.wait_ge(low_ready, NS * (2 * i + k - before) + SPLIT.index(was) + 1)
                        else:
                            dve.wait_ge(mm2_done, PAIRS2 * (2 * i + k - before) + PE_DONE[was])
                    rot = rot_lo[:, k, t:t + 1, :] if t < 4 else rot_hi[:, t - 4:t - 3, :]
                    dve.tensor_tensor(z2[:, t % 4, :, :], x1_arr[:, k, :, :], rot.to_broadcast([P, 2, N]),
                                      op=ALU.mult).then_inc(z2_ready, 1)
                    if t - 1 in SPLIT:
                        low(i, k, SPLIT.index(t - 1))
                    if t == 2 and not last:
                        sum1(i, k + 1)

            def phase(i, k, first=False):
                products1(i, k + 1)
                if not first:
                    sum2(i, k - 1)
                products2(i, k, first=first)

            products1(0, 0, first=True)
            dve.wait_ge(top_here, 112)
            sum1(0, 0)
            phase(0, 0, first=True)
            phase(0, 1)
            with dve.Fori(1, LOOPS) as i:
                phase(i, 0)
                phase(i, 1)
            phase(LOOPS, 0)
            sum2(LOOPS, 0)
            products2(LOOPS, 1, last=True)
            sum2(LOOPS, 1)

        @block.scalar
        def _(act):
            act.wait_ge(w1_here, 80)

            def high5(i, k, first=False):
                act.wait_ge(z5_ready, 2 * i + k + 1)
                if not first:
                    act.wait_ge(mm1_done, 3 * (2 * i + k))
                act.activation(z5_parts[:], z5[:], ACT.Copy).then_inc(z5h_ready, 1)

            def relu1(i, k, first=False):
                act.wait_ge(mm1_done, 3 * (2 * i + k + 1))
                if not first:
                    act.wait_ge(sum1_done, 2 * i + k)
                    act.wait_ge(x1_arr_here[(k + 1) % 2], 16 * ROT * (i + (k + 1) // 2))
                act.activation(x1[:], ps1[:].rearrange("p a n -> p (a n)"), ACT.Relu, bias=b1_sb[:]).then_inc(x1_ready, 1)
                act.wait_ge(x1_ready, 2 * i + k + 1)
                if not first:
                    act.wait_ge(z2_ready, PAIRS2 * (2 * i + k - 1))
                s = k % 2
                for dst, src, n in ((0, 0, 64), (64, 0, 64)):
                    act.dma_start(x1_arr[dst:dst + n, s, 0, :], x1[src:src + n, :]).then_inc(x1_arr_here[s], 16)
                for dst, src, n in ((0, 32, 32), (32, 0, 32), (64, 32, 32), (96, 0, 32)):
                    act.dma_start(x1_arr[dst:dst + n, s, 1, :], x1[src:src + n, :]).then_inc(x1_arr_here[s], 16)

            def relu2(i, k, first=False):
                act.wait_ge(mm2_done, PAIRS2 * (2 * i + k + 1))
                if not first:
                    act.wait_ge(sum2_done, 2 * i + k)
                act.activation(x2[:], ps2[:].rearrange("p a n -> p (a n)"), ACT.Relu, bias=b2_sb[:]).then_inc(x2_ready, 1)

            def highs(i, k, first=False):
                for n, t in enumerate(SPLIT):
                    act.wait_ge(z2_ready, PAIRS2 * (2 * i + k) + t + 1)
                    if n:
                        act.wait_ge(mm2_done, PAIRS2 * (2 * i + k) + PE_DONE[SPLIT[n - 1]])
                    elif not first:
                        act.wait_ge(mm2_done, PAIRS2 * (2 * i + k - 1) + PE_DONE[SPLIT[-1]])
                    act.activation(z2_high[:], z2[:, t % 4, :, :], ACT.Copy).then_inc(high_ready, 1)

            def phase(i, k, first=False):
                high5(i, k + 1)
                if not first:
                    relu2(i, k - 1, first=False)
                relu1(i, k + 1)
                highs(i, k, first=first)

            high5(0, 0, first=True)
            relu1(0, 0, first=True)
            high5(0, 1)
            act.wait_ge(mm1_done, 6)
            act.wait_ge(sum1_done, 1)
            act.wait_ge(x1_arr_here[0], 16 * ROT)
            act.activation(x1[:], ps1[:].rearrange("p a n -> p (a n)"), ACT.Relu, bias=b1_sb[:]).then_inc(x1_ready, 1)
            act.wait_ge(x1_ready, 2)
            for dst, src, n in ((0, 0, 64), (64, 0, 64)):
                act.dma_start(x1_arr[dst:dst + n, 1, 0, :], x1[src:src + n, :]).then_inc(x1_arr_here[1], 16)
            for dst, src, n in ((0, 32, 32), (32, 0, 32), (64, 32, 32), (96, 0, 32)):
                act.dma_start(x1_arr[dst:dst + n, 1, 1, :], x1[src:src + n, :]).then_inc(x1_arr_here[1], 16)
            highs(0, 0, first=True)
            high5(0, 2)
            relu2(0, 0, first=True)
            relu1(0, 2)
            highs(0, 1)
            with act.Fori(1, LOOPS) as i:
                phase(i, 0)
                phase(i, 1)
            phase(LOOPS, 0)
            relu2(LOOPS, 0)
            highs(LOOPS, 1)
            relu2(LOOPS, 1)

            act.wait_ge(top_here, 112)
            for n in range(8):
                half, m = divmod(n, 4)
                act.wait_ge(top_mm, n + 1)
                act.activation(h1[:, m, half * HALF:(half + 1) * HALF], pst[:, n % 4, :], ACT.Relu,
                               bias=bt1_sb[:, m:m + 1]).then_inc(h1_ready, 1)
            for n in range(4):
                half, m = divmod(n, 2)
                act.wait_ge(top_mm, 8 + n + 1)
                act.activation(h2[:, m, half * HALF:(half + 1) * HALF], pst[:, n, :], ACT.Relu,
                               bias=bt2_sb[:, m:m + 1]).then_inc(h2_ready, 1)
            for half in range(2):
                act.wait_ge(top_mm, 12 + half + 1)
                act.activation(y_sb[:, half * HALF:(half + 1) * HALF], pst[0:1, half, :], ACT.Copy).then_inc(y_ready, 1)

        @block.tensor
        def _(pe):
            def layer1(i, k, first=False):
                if not first:
                    pe.wait_ge(x1_ready, 2 * i + k)
                for j in range(PAIRS1):
                    pe.wait_ge(z1_ready, PAIRS1 * (2 * i + k) + j + 1)
                    for a in range(2):
                        for half in range(2):
                            last = pe.matmul(ps1[:, half, :], w1_sb[:, 2 * j + a, :],
                                             z1[:, j, a, half * HALF:(half + 1) * HALF],
                                             start=(j == 0 and a == 0), stop=False)
                    last.then_inc(mm1_done, 1)
                pe.wait_ge(z5_split, 2 * i + k + 1)
                for half in range(2):
                    last = pe.matmul(ps1[:, half, :], w5_parts[:], z5_parts[:, half * HALF:(half + 1) * HALF],
                                     start=False, stop=True)
                last.then_inc(mm1_done, 1)

            def layer2(i, k, first=False):
                if not first:
                    pe.wait_ge(x2_ready, 2 * i + k)
                for t in PE_ORDER:
                    begin, end = t == PE_ORDER[0], t == PE_ORDER[-1]
                    if t in SPLIT:
                        n = SPLIT.index(t)
                        pe.wait_ge(low_ready, NS * (2 * i + k) + n + 1)
                        for a in range(2):
                            for w, z in ((w2_high, z2_high), (w2_low, z2_high), (w2_high, z2_low)):
                                for half in range(2):
                                    last = pe.matmul(ps2[:, half, :], w[:, 2 * n + a, :],
                                                     z[:, a, half * HALF:(half + 1) * HALF], start=False, stop=False)
                    else:
                        pe.wait_ge(z2_ready, PAIRS2 * (2 * i + k) + t + 1)
                        for a in range(2):
                            for half in range(2):
                                last = pe.matmul(ps2[:, half, :], w2_sb[:, 2 * t + a, :],
                                                 z2[:, t % 4, a, half * HALF:(half + 1) * HALF],
                                                 start=(begin and a == 0), stop=(end and a == 1))
                    last.then_inc(mm2_done, 1)

            pe.wait_ge(w1_ready, 1)
            pe.wait_ge(w5_ready, 1)
            pe.wait_ge(w2_ready, NS)
            layer1(0, 0, first=True)
            layer1(0, 1)
            layer2(0, 0, first=True)
            layer1(0, 2)
            layer2(0, 1)
            with pe.Fori(1, LOOPS) as i:
                layer1(i, 1)
                layer2(i, 0)
                layer1(i, 2)
                layer2(i, 1)
            layer1(LOOPS, 1)
            layer2(LOOPS, 0)
            layer2(LOOPS, 1)

            pe.wait_ge(top_here, 112)
            pe.wait_ge(sum1_done, CH)
            pe.wait_ge(sum2_done, CH)
            for n in range(8):
                half, m = divmod(n, 4)
                if n >= 4:
                    pe.wait_ge(h1_ready, n - 3)
                cols = slice(half * HALF, (half + 1) * HALF)
                pe.matmul(pst[:, n % 4, :], wt1a_sb[:, m * P:(m + 1) * P], feat_a[:, cols], start=True, stop=False)
                pe.matmul(pst[:, n % 4, :], wt1b_sb[:, m * P:(m + 1) * P], feat_b[:, cols], start=False,
                          stop=True).then_inc(top_mm, 1)
            for n in range(4):
                half, m = divmod(n, 2)
                pe.wait_ge(h1_ready, 4 + max(n + 1, 4 * half))
                for kt in range(4):
                    last = pe.matmul(pst[:, n, :], wt2_sb[:, kt, m * P:(m + 1) * P],
                                     h1[:, kt, half * HALF:(half + 1) * HALF], start=(kt == 0), stop=(kt == 3))
                last.then_inc(top_mm, 1)
            for half in range(2):
                pe.wait_ge(h2_ready, 2 * half + 2)
                for kt in range(2):
                    last = pe.matmul(pst[0:1, half, :], wt3_sb[:, kt:kt + 1], h2[:, kt, half * HALF:(half + 1) * HALF],
                                     start=(kt == 0), stop=(kt == 1))
                last.then_inc(top_mm, 1)


def layouts(inputs):
    a = {k: np.asarray(v) for k, v in inputs.items()}
    i, k = np.arange(F0), np.arange(REPS)
    out = {}
    out["table"] = np.concatenate([a[f"tbl_{f}"] for f in range(F0)])
    out["ids"] = np.ascontiguousarray(a["ids"].reshape(REPS, B // REPS, F0).transpose(0, 2, 1).reshape(P, B // REPS))
    out["ids"] = np.concatenate([out["ids"], np.zeros((P, JG), out["ids"].dtype)], axis=1)
    first = np.concatenate([[0], np.cumsum(ROWS)[:-1]]).astype(np.int32)
    out["base"] = np.ascontiguousarray(np.broadcast_to(first[None, :, None], (REPS, F0, B // REPS + JG)).reshape(P, -1))
    out["dense"] = np.ascontiguousarray(
        a["dense_ctx"].reshape(2, 2, GROUPS, JG, DENSE).transpose(4, 2, 0, 1, 3).reshape(DENSE, B))
    w1 = a["L0_rec_W1"].reshape(O, F0, F0)
    ii = np.broadcast_to(i[None, None, :], (4, REPS, F0))
    s = np.broadcast_to(4 * np.arange(4)[:, None, None] + k[None, :, None], (4, REPS, F0))
    jj = (ii + s) % F0
    tile = lambda x: np.ascontiguousarray(x.transpose(1, 2, 0, 3).reshape(P, -1, O))
    there = w1[:, ii, jj].transpose(1, 2, 3, 0)
    back = w1[:, jj, ii].transpose(1, 2, 3, 0).copy()
    back[0, 0] = 0
    out["w1a"], out["w1b"] = tile(there), tile(back)
    out["w1c"] = np.ascontiguousarray(np.concatenate([w1[:, i, (i + F0 // 2) % F0].T] * 3))
    w2 = a["L0_rec_W2"].reshape(O, HID, F0)
    t, c, q, u, f = np.ix_(np.arange(PAIRS2), np.arange(2), np.arange(2), np.arange(2), i)
    w2t = w2[:, 32 * (u ^ c) + f + 0 * t + 0 * q, (f + 4 * t + 2 * q + u + 0 * c) % F0]
    out["w2"] = np.ascontiguousarray(w2t.transpose(3, 4, 5, 1, 2, 0).reshape(P, 2 * PAIRS2, O))
    out["b1"], out["b2"] = a["L0_rec_b1"].reshape(P, 1), a["L0_rec_b2"].reshape(P, 1)
    wt1 = a["W_top1"]
    out["wt1a"] = np.ascontiguousarray(wt1[HID:HID + O])
    out["wt1b"] = np.concatenate([wt1[HID + O:], np.zeros((64 - DENSE, TOP1), np.float32), wt1[:HID]])
    out["bt1"] = np.ascontiguousarray(a["b_top1"].reshape(4, P).T)
    out["wt2"] = np.ascontiguousarray(a["W_top2"].reshape(4, P, TOP2).transpose(1, 0, 2))
    out["bt2"] = np.ascontiguousarray(a["b_top2"].reshape(2, P).T)
    out["wt3"] = np.ascontiguousarray(a["W_top3"].reshape(2, P).T)
    return out


def kernel(**inputs):
    import concourse.bacc as bacc
    from concourse.bass_utils import run_bass_kernel_spmd

    nc = bacc.Bacc("TRN2", target_bir_lowering=False, num_devices=1)
    arrays = layouts(inputs)
    args = {name: nc.dram_tensor(f"in_{name}", x.shape, mybir.dt.from_np(x.dtype), kind="ExternalInput").ap()
            for name, x in arrays.items()}
    out = nc.dram_tensor("out_y", (1, B), mybir.dt.float32, kind="ExternalOutput").ap()
    build(nc, y=out, **args)
    r = run_bass_kernel_spmd(nc, [{f"in_{n}": x for n, x in arrays.items()}], core_ids=[0])
    got = r.results[0]["out_y"]
    return np.ascontiguousarray(got.reshape(GROUPS, 2, 2, JG).transpose(1, 2, 0, 3).reshape(B, 1))
```

```python
import numpy as np
import concourse.bass as bass
from concourse import mybir
from contextlib import ExitStack

B, F0, D = 1024, 32, 64
O = 128
HID = 64
DENSE, TOP1, TOP2 = 16, 512, 256
ROWS = [1250, 1000, 125000, 12500, 12500, 125000, 1250, 12500, 125000, 12500, 1250, 1000, 1000, 12500, 1000, 1000,
        1250, 12500, 1000, 12500, 1250, 1000, 12500, 1250, 1000, 1000, 1250, 1250, 1250, 1000, 1000, 1000]

P = 128
N = 1024
HALF = 512
EX = N // D
CH = B // EX
JG = EX // 2
GROUPS = CH // 2
REPS = P // F0
LOOPS = CH // 2 - 1
PAIRS1, PAIRS2 = 2, 8
STORES = 4
ROT = 6

SPLIT = (1, 3, 5)
PE_ORDER = (0, 2, 1, 4, 3, 6, 5, 7)
NS = len(SPLIT)
PE_DONE = {t: PE_ORDER.index(t) + 1 for t in range(PAIRS2)}


def part_slot(k, n):
    return (NS * k + n) % 2


def build(nc, table, ids, base, dense, w1a, w1b, w1c, w2, b1, b2, wt1a, wt1b, bt1, wt2, bt2, wt3, y):
    F32, F32R, I32 = mybir.dt.float32, mybir.dt.float32r, mybir.dt.int32
    ALU, ACT, AX = mybir.AluOpType, mybir.ActivationFunctionType, mybir.AxisListType

    ctx = ExitStack()
    with ctx:
        def sb(name, shape, dt=F32):
            return ctx.enter_context(nc.sbuf_tensor(name, shape, dt))

        def sem(name):
            return ctx.enter_context(nc.semaphore(name))

        scratch = nc.dram_tensor("fields_twice", [CH, 2 * F0, N], F32, kind="Internal").ap()

        ids_sb = sb("ids_sb", [P, B // REPS + JG], I32)
        base_sb = sb("base_sb", [P, B // REPS + JG], I32)
        row_no = sb("row_no", [P, 2, JG], I32)
        gathered = sb("gathered", [P, 2, JG * D])
        fields = sb("fields", [P, 2, N])
        rot_lo = sb("rot_lo", [P, 2, 4, N])
        rot_hi = sb("rot_hi", [P, 4, N])
        x1 = sb("x1", [HID, N])
        x1_arr = sb("x1_arr", [P, 2, 2, N])
        z1 = sb("z1", [P, 2, 2, N])
        z5 = sb("z5", [3 * F0, N])
        z5_parts = sb("z5_parts", [3 * F0, N], F32R)
        z2 = sb("z2", [P, 4, 2, N])
        z2_high = sb("z2_high", [P, 2, 2, N], F32R)
        z2_low = sb("z2_low", [P, 2, 2, N], F32R)
        sums1 = sb("sums1", [P, EX])
        sums2 = sb("sums2", [P, EX])
        w1_sb = sb("w1_sb", [P, 4, O])
        w1b_sb = sb("w1b_sb", [P, 4, O])
        w5_sb = sb("w5_sb", [3 * F0, O])
        w5_parts = sb("w5_parts", [3 * F0, O], F32R)
        w2_sb = sb("w2_sb", [P, 2 * PAIRS2, O])
        w2_high = sb("w2_high", [P, 2 * NS, O], F32R)
        w2_low = sb("w2_low", [P, 2 * NS, O], F32R)
        b1_sb = sb("b1_sb", [P, 1])
        b2_sb = sb("b2_sb", [P, 1])
        feat_a = sb("feat_a", [P, B])
        feat_b = sb("feat_b", [P, B])
        wt1a_sb = sb("wt1a_sb", [P, TOP1])
        wt1b_sb = sb("wt1b_sb", [P, TOP1])
        wt2_sb = sb("wt2_sb", [P, 4, TOP2])
        wt3_sb = sb("wt3_sb", [P, 2])
        bt1_sb = sb("bt1_sb", [P, 4])
        bt2_sb = sb("bt2_sb", [P, 2])
        h1 = z2[:, 0:2, :, :].rearrange("p a b n -> p (a b) n")
        h2 = z2[:, 2, :, :]
        y_sb = z1[0:1, 0, 0, :]

        ps1 = ctx.enter_context(nc.psum_tensor("ps1", [P, 2, HALF], F32))
        ps2 = ctx.enter_context(nc.psum_tensor("ps2", [P, 2, HALF], F32))
        pst = ctx.enter_context(nc.psum_tensor("pst", [P, 4, HALF], F32))

        ids_here = sem("ids_here")
        w1_here, w2_here, top_here = sem("w1_here"), sem("w2_here"), sem("top_here")
        w1_ready, w5_high, w5_ready = sem("w1_ready"), sem("w5_high"), sem("w5_ready")
        w2h_ready, w2_ready = sem("w2h_ready"), sem("w2_ready")
        feat_zero = sem("feat_zero")
        row_ready = sem("row_ready")
        rows_here = [sem(f"rows_here{s}") for s in range(2)]
        stored = sem("stored")
        fields_here = sem("fields_here")
        rot_lo_here = [sem(f"rot_lo_here{s}") for s in range(2)]
        rot_hi_here = sem("rot_hi_here")
        z1_ready, z5_ready, z5h_ready, z5_split = sem("z1_ready"), sem("z5_ready"), sem("z5h_ready"), sem("z5_split")
        z2_ready, high_ready, low_ready = sem("z2_ready"), sem("high_ready"), sem("low_ready")
        mm1_done, mm2_done = sem("mm1_done"), sem("mm2_done")
        x1_ready = sem("x1_ready")
        x1_arr_here = [sem(f"x1_arr_here{s}") for s in range(2)]
        sum1_done, sum2_done = sem("sum1_done"), sem("sum2_done")
        kept1, kept2 = sem("kept1"), sem("kept2")
        top_mm, h1_ready, h2_ready, y_ready, y_stored = (sem("top_mm"), sem("h1_ready"), sem("h2_ready"),
                                                         sem("y_ready"), sem("y_stored"))

        block = ctx.enter_context(nc.Block())

        def window(i, k, first, count):
            return bass.AP(tensor=scratch.tensor, offset=(2 * i + k) * (2 * F0 * N) + first * N,
                           ap=[[N, count], [N, F0], [1, N]])

        def same(i, k, first):
            return bass.AP(tensor=scratch.tensor, offset=(2 * i + k) * (2 * F0 * N) + first * N,
                           ap=[[0, REPS], [N, F0], [1, N]])

        @block.sync
        def _(sp):
            sp.dma_start(ids_sb[:], ids).then_inc(ids_here, 16)
            sp.dma_start(base_sb[:], base).then_inc(ids_here, 16)
            sp.dma_start(w1_sb[:], w1a).then_inc(w1_here, 16)
            sp.dma_start(w1b_sb[:], w1b).then_inc(w1_here, 16)
            sp.dma_start(w5_sb[:], w1c).then_inc(w1_here, 16)
            sp.dma_start(b1_sb[:], b1).then_inc(w1_here, 16)
            sp.dma_start(b2_sb[:], b2).then_inc(w1_here, 16)
            sp.dma_start(w2_sb[:], w2).then_inc(w2_here, 16)

            def load_fields(i, k):
                sp.dma_start(fields[:, 0, :], same(i, k, 0)).then_inc(fields_here, 16)
                sp.dma_start(fields[:, 1, :], same(i, k, F0 // 2)).then_inc(fields_here, 16)

            def load_rot_lo(i, k):
                for t in range(4):
                    sp.dma_start(rot_lo[:, k % 2, t, :], window(i, k, 4 * t, REPS)).then_inc(rot_lo_here[k % 2], 16)

            def load_rot_hi(i, k):
                for t in range(4):
                    sp.dma_start(rot_hi[:, t, :], window(i, k, 4 * t + 16, REPS)).then_inc(rot_hi_here, 16)

            sp.wait_ge(stored, 16 * STORES)
            load_fields(0, 0)
            load_rot_lo(0, 0)
            load_rot_hi(0, 0)
            load_rot_lo(0, 1)
            sp.wait_ge(z1_ready, PAIRS1)
            sp.wait_ge(z5_ready, 1)
            load_fields(0, 1)
            sp.wait_ge(feat_zero, 1)
            sp.dma_start(feat_b[0:DENSE, :], dense).then_inc(top_here, 16)
            for dst, src in ((wt1a_sb, wt1a), (wt1b_sb, wt1b), (wt2_sb, wt2), (wt3_sb, wt3), (bt1_sb, bt1),
                             (bt2_sb, bt2)):
                sp.dma_start(dst[:], src).then_inc(top_here, 16)

            def phase(i, k, last=False):
                if not last:
                    if k == 0:
                        sp.wait_ge(stored, 16 * STORES * (i + 2))
                    sp.wait_ge(z1_ready, PAIRS1 * (2 * i + k + 2))
                    sp.wait_ge(z5_ready, 2 * i + k + 2)
                    load_fields(i, k + 2)
                    sp.wait_ge(z2_ready, PAIRS2 * (2 * i + k) + 4)
                    load_rot_lo(i, k + 2)
                sp.wait_ge(z2_ready, PAIRS2 * (2 * i + k + 1))
                load_rot_hi(i, k + 1)

            with sp.Fori(0, LOOPS) as i:
                phase(i, 0)
                phase(i, 1)
            phase(LOOPS, 0, last=True)
            sp.wait_ge(y_ready, 2)
            sp.dma_start(y, y_sb).then_inc(y_stored, 16)
            sp.wait_ge(y_stored, 16)

        @block.gpsimd
        def _(pool):
            pool.memset(feat_b[:], 0.0).then_inc(feat_zero, 1)
            pool.wait_ge(ids_here, 32)

            def row_numbers(i, s):
                cols = bass.ds((2 * i + s) * JG, JG)
                pool.tensor_tensor(row_no[:, s % 2, :], ids_sb[:, cols], base_sb[:, cols],
                                   op=ALU.add).then_inc(row_ready, 1)

            def group(i, s, first=False):
                for j in range(JG):
                    pool.indirect_dma_start(gathered[:, s, j * D:(j + 1) * D], None, table,
                                            bass.IndirectOffsetOnAxis(ap=row_no[:, s, j:j + 1], axis=0)
                                            ).then_inc(rows_here[s], 16)
                row_numbers(i, s + 1)
                pool.wait_ge(row_ready, 2 * i + s + 2)
                pool.wait_ge(rows_here[s], 16 * JG * (i + 1))
                if not first:
                    pool.wait_ge(stored, 16 * STORES * (2 * i + s))
                for qp in range(2):
                    for copy in range(2):
                        dst = bass.AP(tensor=scratch.tensor,
                                      offset=(2 * i + s) * (4 * F0 * N) + qp * (2 * F0 * N) + copy * (F0 * N),
                                      ap=[[JG * D, 2], [N, F0], [1, JG * D]])
                        pool.dma_start(dst, gathered[64 * qp:64 * qp + 64, s, :]).then_inc(stored, 16)

            row_numbers(0, 0)
            pool.wait_ge(row_ready, 1)
            group(0, 0, first=True)
            group(0, 1)
            with pool.Fori(1, GROUPS // 2) as i:
                group(i, 0)
                group(i, 1)

        @block.vector
        def _(dve):
            dve.wait_ge(w1_here, 80)
            dve.tensor_tensor(w1_sb[:], w1_sb[:], w1b_sb[:], op=ALU.add).then_inc(w1_ready, 1)
            dve.tensor_copy(w5_parts[:], w5_sb[:]).then_inc(w5_high, 1)
            dve.wait_ge(w5_high, 1)
            dve.tensor_tensor(w5_parts[64:96, :], w5_sb[64:96, :], w5_parts[64:96, :].bitcast(F32),
                              op=ALU.subtract).then_inc(w5_ready, 1)
            dve.wait_ge(w2_here, 16)
            for n, t in enumerate(SPLIT):
                dve.tensor_copy(w2_high[:, 2 * n:2 * n + 2, :], w2_sb[:, 2 * t:2 * t + 2, :]).then_inc(w2h_ready, 1)
            for n, t in enumerate(SPLIT):
                dve.wait_ge(w2h_ready, n + 1)
                dve.tensor_tensor(w2_low[:, 2 * n:2 * n + 2, :], w2_sb[:, 2 * t:2 * t + 2, :],
                                  w2_high[:, 2 * n:2 * n + 2, :].bitcast(F32), op=ALU.subtract).then_inc(w2_ready, 1)

            def products1(i, k, first=False):
                dve.wait_ge(fields_here, 32 * (2 * i + k + 1))
                if not first:
                    dve.wait_ge(z5_split, 2 * i + k)
                dve.tensor_tensor(z5[:], fields[0:96, 0, :], fields[0:96, 1, :], op=ALU.mult).then_inc(z5_ready, 1)
                dve.wait_ge(rot_lo_here[k % 2], 64 * (i + k // 2 + 1))
                for j in range(PAIRS1):
                    if not first:
                        dve.wait_ge(mm1_done, 3 * (2 * i + k - 1) + j + 1)
                    dve.tensor_tensor(z1[:, j, :, :], fields[:, 0:1, :].to_broadcast([P, 2, N]),
                                      rot_lo[:, k % 2, 2 * j:2 * j + 2, :], op=ALU.mult).then_inc(z1_ready, 1)
                dve.wait_ge(z5h_ready, 2 * i + k + 1)
                dve.tensor_tensor(z5_parts[32:64, :], z5[32:64, :], z5_parts[32:64, :].bitcast(F32),
                                  op=ALU.subtract).then_inc(z5_split, 1)

            def low(i, k, n):
                dve.wait_ge(high_ready, NS * (2 * i + k) + n + 1)
                slot = part_slot(k, n)
                dve.tensor_tensor(z2_low[:, slot, :, :], z2[:, SPLIT[n] % 4, :, :],
                                  z2_high[:, slot, :, :].bitcast(F32),
                                  op=ALU.subtract).then_inc(low_ready, 1)

            def products2(i, k, first=False):
                dve.wait_ge(x1_arr_here[k], 16 * ROT * (i + 1))
                for t in range(PAIRS2):
                    if t == 4:
                        dve.wait_ge(rot_hi_here, 64 * (2 * i + k + 1))
                    before, was = (0, t - 4) if t >= 4 else (1, t + 4)
                    if not (first and before):
                        if was in SPLIT:
                            dve.wait_ge(low_ready, NS * (2 * i + k - before) + SPLIT.index(was) + 1)
                        else:
                            dve.wait_ge(mm2_done, PAIRS2 * (2 * i + k - before) + PE_DONE[was])
                    rot = rot_lo[:, k, t:t + 1, :] if t < 4 else rot_hi[:, t - 4:t - 3, :]
                    dve.tensor_tensor(z2[:, t % 4, :, :], x1_arr[:, k, :, :], rot.to_broadcast([P, 2, N]),
                                      op=ALU.mult).then_inc(z2_ready, 1)
                    if t - 1 in SPLIT:
                        low(i, k, SPLIT.index(t - 1))

            def phase(i, k, first=False):
                products1(i, k + 1)
                products2(i, k, first=first)

            products1(0, 0, first=True)
            phase(0, 0, first=True)
            phase(0, 1)
            with dve.Fori(1, LOOPS) as i:
                phase(i, 0)
                phase(i, 1)
            phase(LOOPS, 0)
            products2(LOOPS, 1)

        @block.scalar
        def _(act):
            act.wait_ge(w1_here, 80)

            def high5(i, k, first=False):
                act.wait_ge(z5_ready, 2 * i + k + 1)
                if not first:
                    act.wait_ge(mm1_done, 3 * (2 * i + k))
                act.activation(z5_parts[:], z5[:], ACT.Copy).then_inc(z5h_ready, 1)

            def relu1(i, k, first=False, early=False):
                act.wait_ge(mm1_done, 3 * (2 * i + k + 1))
                if not first:
                    act.wait_ge(x1_arr_here[(k + 1) % 2], 16 * ROT * (i + (k + 1) // 2))
                act.activation(x1[:], ps1[0:HID].rearrange("p a n -> p (a n)"), ACT.Relu,
                               bias=b1_sb[0:HID]).then_inc(x1_ready, 1)
                act.wait_ge(x1_ready, 2 * i + k + 1)
                if not first and not early:
                    act.wait_ge(z2_ready, PAIRS2 * (2 * i + k - 1))
                s = k % 2
                for dst, src, n in ((0, 0, 64), (64, 0, 64)):
                    act.dma_start(x1_arr[dst:dst + n, s, 0, :], x1[src:src + n, :]).then_inc(x1_arr_here[s], 16)
                for dst, src, n in ((0, 32, 32), (32, 0, 32), (64, 32, 32), (96, 0, 32)):
                    act.dma_start(x1_arr[dst:dst + n, s, 1, :], x1[src:src + n, :]).then_inc(x1_arr_here[s], 16)

            def relu_sums(ps, bias, sums, rows, examples):
                for e in examples:
                    half, at = divmod(e * D, HALF)
                    last = act.activation(ps[rows, half, at:at + D], ps[rows, half, at:at + D], ACT.Relu, bias=bias[rows, :],
                                          accum_out=sums[rows, e:e + 1])
                return last

            def sum1(i, k, part):
                rows = slice(HID, P)
                last = relu_sums(ps1, b1_sb, sums1, rows, range(part * EX // 2, (part + 1) * EX // 2))
                if part:
                    last.then_inc(sum1_done, 1)
                    act.wait_ge(sum1_done, 2 * i + k + 1)
                    act.activation(feat_b[rows, bass.ds((2 * i + k) * EX, EX)], sums1[rows, :],
                                   ACT.Copy).then_inc(kept1, 1)

            def sum2(i, k):
                act.wait_ge(mm2_done, PAIRS2 * (2 * i + k + 1))
                rows = slice(0, P)
                relu_sums(ps2, b2_sb, sums2, rows, range(EX)).then_inc(sum2_done, 1)
                act.wait_ge(sum2_done, 2 * i + k + 1)
                act.activation(feat_a[:, bass.ds((2 * i + k) * EX, EX)], sums2[:], ACT.Copy).then_inc(kept2, 1)

            def highs(i, k, which, first=False):
                for n in which:
                    t = SPLIT[n]
                    act.wait_ge(z2_ready, PAIRS2 * (2 * i + k) + t + 1)
                    if n >= 2:
                        act.wait_ge(mm2_done, PAIRS2 * (2 * i + k) + PE_DONE[SPLIT[n - 2]])
                    elif not first:
                        act.wait_ge(mm2_done, PAIRS2 * (2 * i + k - 1) + PE_DONE[SPLIT[NS - 2 + n]])
                    act.activation(z2_high[:, part_slot(k, n), :, :], z2[:, t % 4, :, :], ACT.Copy).then_inc(high_ready, 1)

            def phase(i, k, first=False, early=False):
                high5(i, k + 1)
                if not first:
                    sum2(i, k - 1)
                highs(i, k, (0,), first=first)
                relu1(i, k + 1, early=early)
                sum1(i, k + 1, 0)
                highs(i, k, (1,), first=first)
                sum1(i, k + 1, 1)
                highs(i, k, range(2, NS))

            high5(0, 0, first=True)
            relu1(0, 0, first=True)
            act.wait_ge(top_here, 112)
            sum1(0, 0, 0)
            sum1(0, 0, 1)
            phase(0, 0, first=True, early=True)
            phase(0, 1)
            with act.Fori(1, LOOPS) as i:
                phase(i, 0)
                phase(i, 1)
            phase(LOOPS, 0)
            sum2(LOOPS, 0)
            highs(LOOPS, 1, range(NS))
            sum2(LOOPS, 1)

            act.wait_ge(top_here, 112)
            for n in range(8):
                half, m = divmod(n, 4)
                act.wait_ge(top_mm, n + 1)
                act.activation(h1[:, m, half * HALF:(half + 1) * HALF], pst[:, n % 4, :], ACT.Relu,
                               bias=bt1_sb[:, m:m + 1]).then_inc(h1_ready, 1)
            for n in range(4):
                half, m = divmod(n, 2)
                act.wait_ge(top_mm, 8 + n + 1)
                act.activation(h2[:, m, half * HALF:(half + 1) * HALF], pst[:, n, :], ACT.Relu,
                               bias=bt2_sb[:, m:m + 1]).then_inc(h2_ready, 1)
            for half in range(2):
                act.wait_ge(top_mm, 12 + half + 1)
                act.activation(y_sb[:, half * HALF:(half + 1) * HALF], pst[0:1, half, :], ACT.Copy).then_inc(y_ready, 1)

        @block.tensor
        def _(pe):
            def layer1(i, k, first=False):
                if not first:
                    pe.wait_ge(sum1_done, 2 * i + k)
                for j in range(PAIRS1):
                    pe.wait_ge(z1_ready, PAIRS1 * (2 * i + k) + j + 1)
                    for a in range(2):
                        for half in range(2):
                            last = pe.matmul(ps1[:, half, :], w1_sb[:, 2 * j + a, :],
                                             z1[:, j, a, half * HALF:(half + 1) * HALF],
                                             start=(j == 0 and a == 0), stop=False)
                    last.then_inc(mm1_done, 1)
                pe.wait_ge(z5_split, 2 * i + k + 1)
                for half in range(2):
                    last = pe.matmul(ps1[:, half, :], w5_parts[:], z5_parts[:, half * HALF:(half + 1) * HALF],
                                     start=False, stop=True)
                last.then_inc(mm1_done, 1)

            def layer2(i, k, first=False):
                if not first:
                    pe.wait_ge(sum2_done, 2 * i + k)
                for t in PE_ORDER:
                    begin, end = t == PE_ORDER[0], t == PE_ORDER[-1]
                    if t in SPLIT:
                        n = SPLIT.index(t)
                        pe.wait_ge(low_ready, NS * (2 * i + k) + n + 1)
                        for a in range(2):
                            for w, z in ((w2_high, z2_high), (w2_low, z2_high), (w2_high, z2_low)):
                                for half in range(2):
                                    last = pe.matmul(ps2[:, half, :], w[:, 2 * n + a, :],
                                                     z[:, part_slot(k, n), a, half * HALF:(half + 1) * HALF],
                                                     start=False, stop=False)
                    else:
                        pe.wait_ge(z2_ready, PAIRS2 * (2 * i + k) + t + 1)
                        for a in range(2):
                            for half in range(2):
                                last = pe.matmul(ps2[:, half, :], w2_sb[:, 2 * t + a, :],
                                                 z2[:, t % 4, a, half * HALF:(half + 1) * HALF],
                                                 start=(begin and a == 0), stop=(end and a == 1))
                    last.then_inc(mm2_done, 1)

            pe.wait_ge(w1_ready, 1)
            pe.wait_ge(w5_ready, 1)
            pe.wait_ge(w2_ready, NS)
            layer1(0, 0, first=True)
            layer1(0, 1)
            layer2(0, 0, first=True)
            layer1(0, 2)
            layer2(0, 1)
            with pe.Fori(1, LOOPS) as i:
                layer1(i, 1)
                layer2(i, 0)
                layer1(i, 2)
                layer2(i, 1)
            layer1(LOOPS, 1)
            layer2(LOOPS, 0)
            layer2(LOOPS, 1)

            pe.wait_ge(top_here, 112)
            pe.wait_ge(kept1, CH)
            pe.wait_ge(kept2, CH)
            for n in range(8):
                half, m = divmod(n, 4)
                if n >= 4:
                    pe.wait_ge(h1_ready, n - 3)
                cols = slice(half * HALF, (half + 1) * HALF)
                pe.matmul(pst[:, n % 4, :], wt1a_sb[:, m * P:(m + 1) * P], feat_a[:, cols], start=True, stop=False)
                pe.matmul(pst[:, n % 4, :], wt1b_sb[:, m * P:(m + 1) * P], feat_b[:, cols], start=False,
                          stop=True).then_inc(top_mm, 1)
            for n in range(4):
                half, m = divmod(n, 2)
                pe.wait_ge(h1_ready, 4 + max(n + 1, 4 * half))
                for kt in range(4):
                    last = pe.matmul(pst[:, n, :], wt2_sb[:, kt, m * P:(m + 1) * P],
                                     h1[:, kt, half * HALF:(half + 1) * HALF], start=(kt == 0), stop=(kt == 3))
                last.then_inc(top_mm, 1)
            for half in range(2):
                pe.wait_ge(h2_ready, 2 * half + 2)
                for kt in range(2):
                    last = pe.matmul(pst[0:1, half, :], wt3_sb[:, kt:kt + 1], h2[:, kt, half * HALF:(half + 1) * HALF],
                                     start=(kt == 0), stop=(kt == 1))
                last.then_inc(top_mm, 1)


def layouts(inputs):
    a = {k: np.asarray(v) for k, v in inputs.items()}
    i, k = np.arange(F0), np.arange(REPS)
    out = {}
    out["table"] = np.concatenate([a[f"tbl_{f}"] for f in range(F0)])
    out["ids"] = np.ascontiguousarray(a["ids"].reshape(REPS, B // REPS, F0).transpose(0, 2, 1).reshape(P, B // REPS))
    out["ids"] = np.concatenate([out["ids"], np.zeros((P, JG), out["ids"].dtype)], axis=1)
    first = np.concatenate([[0], np.cumsum(ROWS)[:-1]]).astype(np.int32)
    out["base"] = np.ascontiguousarray(np.broadcast_to(first[None, :, None], (REPS, F0, B // REPS + JG)).reshape(P, -1))
    out["dense"] = np.ascontiguousarray(
        a["dense_ctx"].reshape(2, 2, GROUPS, JG, DENSE).transpose(4, 2, 0, 1, 3).reshape(DENSE, B))
    w1 = a["L0_rec_W1"].reshape(O, F0, F0)
    ii = np.broadcast_to(i[None, None, :], (4, REPS, F0))
    s = np.broadcast_to(4 * np.arange(4)[:, None, None] + k[None, :, None], (4, REPS, F0))
    jj = (ii + s) % F0
    tile = lambda x: np.ascontiguousarray(x.transpose(1, 2, 0, 3).reshape(P, -1, O))
    there = w1[:, ii, jj].transpose(1, 2, 3, 0)
    back = w1[:, jj, ii].transpose(1, 2, 3, 0).copy()
    back[0, 0] = 0
    out["w1a"], out["w1b"] = tile(there), tile(back)
    out["w1c"] = np.ascontiguousarray(np.concatenate([w1[:, i, (i + F0 // 2) % F0].T] * 3))
    w2 = a["L0_rec_W2"].reshape(O, HID, F0)
    t, c, q, u, f = np.ix_(np.arange(PAIRS2), np.arange(2), np.arange(2), np.arange(2), i)
    w2t = w2[:, 32 * (u ^ c) + f + 0 * t + 0 * q, (f + 4 * t + 2 * q + u + 0 * c) % F0]
    out["w2"] = np.ascontiguousarray(w2t.transpose(3, 4, 5, 1, 2, 0).reshape(P, 2 * PAIRS2, O))
    out["b1"], out["b2"] = a["L0_rec_b1"].reshape(P, 1), a["L0_rec_b2"].reshape(P, 1)
    wt1 = a["W_top1"]
    out["wt1a"] = np.ascontiguousarray(wt1[HID:HID + O])
    out["wt1b"] = np.concatenate([wt1[HID + O:], np.zeros((64 - DENSE, TOP1), np.float32), wt1[:HID]])
    out["bt1"] = np.ascontiguousarray(a["b_top1"].reshape(4, P).T)
    out["wt2"] = np.ascontiguousarray(a["W_top2"].reshape(4, P, TOP2).transpose(1, 0, 2))
    out["bt2"] = np.ascontiguousarray(a["b_top2"].reshape(2, P).T)
    out["wt3"] = np.ascontiguousarray(a["W_top3"].reshape(2, P).T)
    return out


def kernel(**inputs):
    import concourse.bacc as bacc
    from concourse.bass_utils import run_bass_kernel_spmd

    nc = bacc.Bacc("TRN2", target_bir_lowering=False, num_devices=1)
    arrays = layouts(inputs)
    args = {name: nc.dram_tensor(f"in_{name}", x.shape, mybir.dt.from_np(x.dtype), kind="ExternalInput").ap()
            for name, x in arrays.items()}
    out = nc.dram_tensor("out_y", (1, B), mybir.dt.float32, kind="ExternalOutput").ap()
    build(nc, y=out, **args)
    r = run_bass_kernel_spmd(nc, [{f"in_{n}": x for n, x in arrays.items()}], core_ids=[0])
    got = r.results[0]["out_y"]
    return np.ascontiguousarray(got.reshape(GROUPS, 2, 2, JG).transpose(1, 2, 0, 3).reshape(B, 1))
```

```python
import numpy as np
import concourse.bass as bass
from concourse import mybir
from contextlib import ExitStack

B, F0, D = 1024, 32, 64
O = 128
HID = 64
DENSE, TOP1, TOP2 = 16, 512, 256
ROWS = [1250, 1000, 125000, 12500, 12500, 125000, 1250, 12500, 125000, 12500, 1250, 1000, 1000, 12500, 1000, 1000,
        1250, 12500, 1000, 12500, 1250, 1000, 12500, 1250, 1000, 1000, 1250, 1250, 1250, 1000, 1000, 1000]

P = 128
N = 1024
HALF = 512
EX = N // D
CH = B // EX
JG = EX // 2
GROUPS = CH // 2
REPS = P // F0
LOOPS = CH // 2 - 1
PAIRS1, PAIRS2 = 2, 8
APART = F0 // 2
KEPT = F0 + APART
STORES = 4

TILE = (0, 1, 0, 1, 2, 2, 3, 3)
ARR = (0, 0, 1, 1, 0, 1, 0, 1)
SPLIT = (2, 4, 6)
PE_ORDER = (0, 1, 3, 2, 5, 4, 7, 6)
FULL = tuple(p for p in range(PAIRS2) if p not in SPLIT)
NS = len(SPLIT)
SLOTS = 2
TOP_STEPS = 7
TILE_READ = [max(p for p in range(PAIRS2) if TILE[p] == t) + 1 for t in range(4)]
PE_DONE = [PE_ORDER.index(p) + 1 for p in range(PAIRS2)]


def exists(i, k, back):
    return not isinstance(i, int) or 2 * i + k >= back


def part_slot(k, n):
    return (NS * k + n) % SLOTS


def build(nc, table, ids, base, dense, w1a, w1b, w1c, w5_minus, w2, b1, b2, wt1a, wt1b, bt1, wt2, bt2, wt3, y):
    F32, F32R, I32 = mybir.dt.float32, mybir.dt.float32r, mybir.dt.int32
    ALU, ACT = mybir.AluOpType, mybir.ActivationFunctionType

    ctx = ExitStack()
    with ctx:
        def sb(name, shape, dt=F32):
            return ctx.enter_context(nc.sbuf_tensor(name, shape, dt))

        def sem(name):
            return ctx.enter_context(nc.semaphore(name))

        scratch = nc.dram_tensor("field_rows", [CH, KEPT, N], F32, kind="Internal").ap()

        ids_sb = sb("ids_sb", [P, B // REPS + JG], I32)
        base_sb = sb("base_sb", [P, B // REPS + JG], I32)
        row_no = sb("row_no", [P, JG], I32)
        gathered = sb("gathered", [P, JG * D])
        fields = sb("fields", [P, 2, N])
        rot = sb("rot", [P, 2, 4, N])
        x1 = sb("x1", [HID, N])
        x1_arr = sb("x1_arr", [P, 2, 4, N])
        z1 = sb("z1", [P, 2, 2, N])
        z5 = sb("z5", [64, N])
        z5_parts = sb("z5_parts", [P, N], F32R)
        z2 = sb("z2", [P, 4, 2, N])
        z2_high = sb("z2_high", [P, SLOTS, 2, N], F32R)
        z2_low = sb("z2_low", [P, SLOTS, 2, N], F32R)
        sums1 = sb("sums1", [P, EX])
        sums2 = sb("sums2", [P, EX])
        w1_sb = sb("w1_sb", [P, 4, O])
        w5_minus_sb = sb("w5_minus_sb", [P, 1])
        w5_parts = sb("w5_parts", [P, O], F32R)
        w2_sb = sb("w2_sb", [P, 2 * len(FULL), O])
        w2_high = sb("w2_high", [P, 2 * NS, O], F32R)
        w2_low = sb("w2_low", [P, 2 * NS, O], F32R)
        b1_sb = sb("b1_sb", [P, 1])
        b2_sb = sb("b2_sb", [P, 1])
        feat_a = sb("feat_a", [P, B])
        feat_b = sb("feat_b", [P, B])
        wt1a_sb = sb("wt1a_sb", [P, TOP1])
        wt1b_sb = sb("wt1b_sb", [P, TOP1])
        wt2_sb = sb("wt2_sb", [P, 4, TOP2])
        wt3_sb = sb("wt3_sb", [P, 2])
        bt1_sb = sb("bt1_sb", [P, 4])
        bt2_sb = sb("bt2_sb", [P, 2])
        h1 = z2[:, 0:2, :, :].rearrange("p a b n -> p (a b) n")
        h2 = z2[:, 2, :, :]
        staged = z2[:, 0, :, :].rearrange("p a n -> p (a n)")
        w2_all = staged[:, 0:2 * PAIRS2 * O].rearrange("p (t o) -> p t o", o=O)
        staged = z2[:, 1, 0, :]
        w1b_sb = staged[:, 0:4 * O].rearrange("p (t o) -> p t o", o=O)
        w5_sb = z2[:, 1, 1, 0:O]
        w5_high = z2_high[:, 0, 0, 0:O]
        y_sb = z1[0:1, 0, 0, :]

        ps1 = [ctx.enter_context(nc.psum_tensor(f"ps1_{s}", [P, 2, HALF], F32)) for s in range(2)]
        ps2 = [ctx.enter_context(nc.psum_tensor(f"ps2_{s}", [P, 2, HALF], F32)) for s in range(2)]
        top_banks = [ps1[0][:, 0, :], ps1[0][:, 1, :], ps1[1][:, 0, :], ps1[1][:, 1, :]]

        ids_here = sem("ids_here")
        w1_here, w2_here, top_here = sem("w1_here"), sem("w2_here"), sem("top_here")
        w1_ready, w5h_ready, w5_ready = sem("w1_ready"), sem("w5h_ready"), sem("w5_ready")
        w2h_ready, w2_ready = sem("w2h_ready"), sem("w2_ready")
        feat_zero = sem("feat_zero")
        row_ready = sem("row_ready")
        rows_here = sem("rows_here")
        stored0, stored = sem("stored0"), sem("stored")
        fields_here = sem("fields_here")
        rot_here = [[sem(f"rot_here{s}_{j}") for j in range(2)] for s in range(2)]
        z1_ready, z5_ready, z5h_ready, z5_split = sem("z1_ready"), sem("z5_ready"), sem("z5h_ready"), sem("z5_split")
        z2_ready, high_ready = sem("z2_ready"), sem("high_ready")
        low_ready = sem("low_ready")
        mm1_done, mm2_done = sem("mm1_done"), sem("mm2_done")
        x1_ready = sem("x1_ready")
        x1_arr_here = [[sem(f"x1_arr_here{s}_{cp}") for cp in range(2)] for s in range(2)]
        sum1_done, sum2_done = sem("sum1_done"), sem("sum2_done")
        kept1, kept2 = sem("kept1"), sem("kept2")
        top_mm, h1_ready, h2_ready, y_ready, y_stored = (sem("top_mm"), sem("h1_ready"), sem("h2_ready"),
                                                         sem("y_ready"), sem("y_stored"))

        block = ctx.enter_context(nc.Block())

        def window(i, k, first, count=F0, step=N):
            return bass.AP(tensor=scratch.tensor, offset=(2 * i + k) * (KEPT * N) + first * N,
                           ap=[[N, count], [step, REPS], [1, N]])

        def store(queue, g, qp, again, done):
            rows, first = (2 * APART, F0) if again else (2 * F0, 0)
            dst = bass.AP(tensor=scratch.tensor, offset=g * (2 * KEPT * N) + qp * (KEPT * N) + first * N,
                          ap=[[JG * D, rows], [1, JG * D]])
            queue.dma_start(dst, gathered[64 * qp:64 * qp + rows, :]).then_inc(done, 16)

        def repeated(first, count):
            return x1[first:first + count, :].unsqueeze(1).to_broadcast([count, REPS, N])

        @block.sync
        def _(sp):
            sp.dma_start(ids_sb[:], ids).then_inc(ids_here, 16)
            sp.dma_start(base_sb[:], base).then_inc(ids_here, 16)
            sp.dma_start(w1_sb[:], w1a).then_inc(w1_here, 16)
            sp.dma_start(w1b_sb, w1b).then_inc(w1_here, 16)
            sp.dma_start(w5_sb, w1c).then_inc(w1_here, 16)
            sp.dma_start(w5_minus_sb[:], w5_minus).then_inc(w1_here, 16)
            sp.dma_start(b1_sb[:], b1).then_inc(w1_here, 16)
            sp.dma_start(b2_sb[:], b2).then_inc(w1_here, 16)
            sp.dma_start(w2_all, w2).then_inc(w2_here, 16)

            sp.wait_ge(feat_zero, 1)
            sp.dma_start(feat_b[0:DENSE, :], dense).then_inc(top_here, 16)
            for dst, src in ((wt1a_sb, wt1a), (wt1b_sb, wt1b), (wt2_sb, wt2), (wt3_sb, wt3), (bt1_sb, bt1),
                             (bt2_sb, bt2)):
                sp.dma_start(dst[:], src).then_inc(top_here, 16)

            def load_fields(i, k, dst=fields):
                sp.dma_start(dst[:, 0, :], window(i, k, 0, step=0)).then_inc(fields_here, 16)
                sp.dma_start(dst[0:64, 1, :], window(i, k, APART, count=APART, step=0)).then_inc(fields_here, 16)

            def load_rot(i, k, t):
                sp.dma_start(rot[:, k % 2, t, :], window(i, k, 4 * t)).then_inc(rot_here[k % 2][t // 2], 16)

            sp.wait_ge(rows_here, 16 * JG)
            for qp in range(2):
                for again in range(2):
                    store(sp, 0, qp, again, stored0)
            sp.wait_ge(stored0, 16 * STORES)
            load_fields(0, 0)
            for t in range(4):
                load_rot(0, 0, t)
            sp.wait_ge(fields_here, 32)
            load_fields(0, 1, dst=x1_arr[:, 1, 0:2, :])
            for t in range(4):
                load_rot(0, 1, t)

            def phase(i, k):
                if k == 0:
                    sp.wait_ge(stored, 16 * STORES * (i + 1))
                sp.wait_ge(z1_ready, PAIRS1 * (2 * i + k + 2))
                sp.wait_ge(z5_ready, 2 * i + k + 2)
                load_fields(i, k + 2)
                for t in range(4):
                    sp.wait_ge(z2_ready, PAIRS2 * (2 * i + k) + TILE_READ[t])
                    load_rot(i, k + 2, t)

            with sp.Fori(0, LOOPS) as i:
                phase(i, 0)
                phase(i, 1)
            sp.wait_ge(y_ready, 2)
            sp.dma_start(y, y_sb).then_inc(y_stored, 16)
            sp.wait_ge(y_stored, 16)

        @block.gpsimd
        def _(pool):
            pool.memset(feat_b[:], 0.0).then_inc(feat_zero, 1)
            pool.wait_ge(ids_here, 32)

            def row_numbers(g):
                cols = bass.ds(g * JG, JG)
                pool.tensor_tensor(row_no[:], ids_sb[:, cols], base_sb[:, cols], op=ALU.add).then_inc(row_ready, 1)
                pool.wait_ge(row_ready, g + 1)

            def gathers():
                for j in range(JG):
                    pool.indirect_dma_start(gathered[:, j * D:(j + 1) * D], None, table,
                                            bass.IndirectOffsetOnAxis(ap=row_no[:, j:j + 1], axis=0)
                                            ).then_inc(rows_here, 16)

            row_numbers(0)
            gathers()
            pool.wait_ge(stored0, 16 * STORES)
            row_numbers(1)
            with pool.Fori(1, GROUPS) as g:
                gathers()
                pool.wait_ge(rows_here, 16 * JG * (g + 1))
                for qp in range(2):
                    for again in range(2):
                        store(pool, g, qp, again, stored)
                pool.wait_ge(stored, 16 * STORES * g)
                row_numbers(g + 1)

        @block.vector
        def _(dve):
            dve.wait_ge(w1_here, 96)
            dve.tensor_tensor(w1_sb[:], w1_sb[:], w1b_sb, op=ALU.add).then_inc(w1_ready, 1)
            dve.tensor_copy(w5_high, w5_sb).then_inc(w5h_ready, 1)
            dve.wait_ge(w5h_ready, 1)
            dve.scalar_tensor_tensor(w5_parts[:], w5_high.bitcast(F32), w5_minus_sb[:], w5_sb, op0=ALU.mult,
                                     op1=ALU.add).then_inc(w5_ready, 1)
            dve.wait_ge(w2_here, 16)
            for n, p in enumerate(FULL):
                dve.tensor_copy(w2_sb[:, 2 * n:2 * n + 2, :], w2_all[:, 2 * p:2 * p + 2, :]).then_inc(w2_ready, 1)
            for n, p in enumerate(SPLIT):
                dve.tensor_copy(w2_high[:, 2 * n:2 * n + 2, :], w2_all[:, 2 * p:2 * p + 2, :]).then_inc(w2h_ready, 1)
            for n, p in enumerate(SPLIT):
                dve.wait_ge(w2h_ready, n + 1)
                dve.tensor_tensor(w2_low[:, 2 * n:2 * n + 2, :], w2_all[:, 2 * p:2 * p + 2, :],
                                  w2_high[:, 2 * n:2 * n + 2, :].bitcast(F32), op=ALU.subtract).then_inc(w2_ready, 1)
            dve.wait_ge(w2_ready, PAIRS2)
            dve.wait_ge(w5_ready, 1)

            def source(i, k):
                return x1_arr[:, 1, :, :] if isinstance(i, int) and 2 * i + k == 1 else fields

            def products16(i, k):
                src = source(i, k)
                dve.wait_ge(fields_here, 32 * (2 * i + k + 1))
                if exists(i, k, 1):
                    dve.wait_ge(z5_split, 2 * i + k)
                dve.tensor_tensor(z5[:], src[0:64, 0, :], src[0:64, 1, :], op=ALU.mult).then_inc(z5_ready, 1)

            def products1(i, k, j):
                src = source(i, k)
                dve.wait_ge(rot_here[k % 2][j], 32 * (i + k // 2 + 1))
                if exists(i, k, 1):
                    dve.wait_ge(mm1_done, 3 * (2 * i + k - 1) + j + 1)
                dve.tensor_tensor(z1[:, j, :, :], src[:, 0:1, :].to_broadcast([P, 2, N]),
                                  rot[:, k % 2, 2 * j:2 * j + 2, :], op=ALU.mult).then_inc(z1_ready, 1)

            def low16(i, k):
                dve.wait_ge(z5h_ready, 2 * i + k + 1)
                dve.tensor_tensor(z5_parts[64:128, :], z5[:], z5_parts[0:64, :].bitcast(F32),
                                  op=ALU.subtract).then_inc(z5_split, 1)

            def low(i, k, n):
                dve.wait_ge(high_ready, NS * (2 * i + k) + n + 1)
                slot = part_slot(k, n)
                dve.tensor_tensor(z2_low[:, slot, :, :], z2[:, SPLIT[n] % 4, :, :],
                                  z2_high[:, slot, :, :].bitcast(F32), op=ALU.subtract).then_inc(low_ready, 1)

            def products2(i, k, p):
                if p in (ARR.index(0), ARR.index(1)):
                    dve.wait_ge(x1_arr_here[k][ARR[p]], (32, 64)[ARR[p]] * (i + 1))
                before, was = (0, p - 4) if p >= 4 else (1, p + 4)
                if exists(i, k, before):
                    if was in SPLIT:
                        dve.wait_ge(low_ready, NS * (2 * i + k - before) + SPLIT.index(was) + 1)
                    else:
                        dve.wait_ge(mm2_done, PAIRS2 * (2 * i + k - before) + PE_DONE[was])
                dve.tensor_tensor(z2[:, p % 4, :, :], x1_arr[:, k, 2 * ARR[p]:2 * ARR[p] + 2, :],
                                  rot[:, k, TILE[p]:TILE[p] + 1, :].to_broadcast([P, 2, N]),
                                  op=ALU.mult).then_inc(z2_ready, 1)
                if p - 1 in SPLIT:
                    low(i, k, SPLIT.index(p - 1))

            def phase(i, k):
                products16(i, k + 1)
                products1(i, k + 1, 0)
                products2(i, k, 0)
                products2(i, k, 1)
                products1(i, k + 1, 1)
                low16(i, k + 1)
                for p in range(2, PAIRS2):
                    products2(i, k, p)

            products16(0, 0)
            products1(0, 0, 0)
            products1(0, 0, 1)
            low16(0, 0)
            phase(0, 0)
            phase(0, 1)
            with dve.Fori(1, LOOPS) as i:
                phase(i, 0)
                phase(i, 1)
            phase(LOOPS, 0)
            for p in range(PAIRS2):
                products2(LOOPS, 1, p)

        @block.scalar
        def _(act):
            act.wait_ge(w1_here, 96)

            def high16(i, k):
                act.wait_ge(z5_ready, 2 * i + k + 1)
                if exists(i, k, 1):
                    act.wait_ge(mm1_done, 3 * (2 * i + k))
                act.activation(z5_parts[0:64, :], z5[:], ACT.Copy).then_inc(z5h_ready, 1)

            def relu1(i, k):
                act.wait_ge(mm1_done, 3 * (2 * i + k + 1))
                if exists(i, k, 1):
                    for cp in range(2):
                        act.wait_ge(x1_arr_here[(k + 1) % 2][cp], (32, 64)[cp] * (i + (k + 1) // 2))
                act.activation(x1[:], ps1[k % 2][0:HID].rearrange("p a n -> p (a n)"), ACT.Relu,
                               bias=b1_sb[0:HID]).then_inc(x1_ready, 1)
                act.wait_ge(x1_ready, 2 * i + k + 1)
                if exists(i, k, 2):
                    act.wait_ge(z2_ready, PAIRS2 * (2 * i + k - 1))
                s = k % 2
                for u in range(2):
                    act.dma_start(x1_arr[:, s, u, :], repeated(32 * u, 32)).then_inc(x1_arr_here[s][0], 16)
                for u in range(2):
                    for r in range(2):
                        act.dma_start(x1_arr[64 * r:64 * r + 64, s, 2 + u, :],
                                      repeated(32 * u + 16 * (1 - r), 16)).then_inc(x1_arr_here[s][1], 16)

            def relu_sums(ps, bias, sums, rows):
                for e in range(EX):
                    half, at = divmod(e * D, HALF)
                    last = act.activation(ps[rows, half, at:at + D], ps[rows, half, at:at + D], ACT.Relu,
                                          bias=bias[rows, :],
                                          accum_out=sums[rows, e:e + 1])
                return last

            def sum1(i, k):
                rows = slice(HID, P)
                relu_sums(ps1[k % 2], b1_sb, sums1, rows).then_inc(sum1_done, 1)
                act.wait_ge(sum1_done, 2 * i + k + 1)
                act.activation(feat_b[rows, bass.ds((2 * i + k) * EX, EX)], sums1[rows, :],
                               ACT.Copy).then_inc(kept1, 1)

            def sum2(i, k):
                act.wait_ge(mm2_done, PAIRS2 * (2 * i + k + 1))
                rows = slice(0, P)
                relu_sums(ps2[k % 2], b2_sb, sums2, rows).then_inc(sum2_done, 1)
                act.wait_ge(sum2_done, 2 * i + k + 1)
                act.activation(feat_a[:, bass.ds((2 * i + k) * EX, EX)], sums2[:], ACT.Copy).then_inc(kept2, 1)

            def high(i, k, n):
                p = SPLIT[n]
                act.wait_ge(z2_ready, PAIRS2 * (2 * i + k) + p + 1)
                if n >= SLOTS:
                    act.wait_ge(mm2_done, PAIRS2 * (2 * i + k) + PE_DONE[SPLIT[n - SLOTS]])
                elif exists(i, k, 1):
                    act.wait_ge(mm2_done, PAIRS2 * (2 * i + k - 1) + PE_DONE[SPLIT[NS - SLOTS + n]])
                act.activation(z2_high[:, part_slot(k, n), :, :], z2[:, p % 4, :, :], ACT.Copy).then_inc(high_ready, 1)

            def phase(i, k):
                high16(i, k + 1)
                if exists(i, k, 1):
                    sum2(i, k - 1)
                high(i, k, 0)
                relu1(i, k + 1)
                high(i, k, 1)
                sum1(i, k + 1)
                high(i, k, 2)

            high16(0, 0)
            relu1(0, 0)
            act.wait_ge(top_here, 112)
            sum1(0, 0)
            phase(0, 0)
            phase(0, 1)
            with act.Fori(1, LOOPS) as i:
                phase(i, 0)
                phase(i, 1)
            phase(LOOPS, 0)
            sum2(LOOPS, 0)
            for n in range(NS):
                high(LOOPS, 1, n)

            act.wait_ge(top_here, 112)
            for half in range(2):
                cols = slice(half * HALF, (half + 1) * HALF)
                if half == 0:
                    sum2(LOOPS, 1)
                for m in range(4):
                    act.wait_ge(top_mm, TOP_STEPS * half + m + 1)
                    act.activation(h1[:, m, cols], top_banks[m], ACT.Relu,
                                   bias=bt1_sb[:, m:m + 1]).then_inc(h1_ready, 1)
                for m in range(2):
                    act.wait_ge(top_mm, TOP_STEPS * half + 4 + m + 1)
                    act.activation(h2[:, m, cols], top_banks[m], ACT.Relu,
                                   bias=bt2_sb[:, m:m + 1]).then_inc(h2_ready, 1)
                act.wait_ge(top_mm, TOP_STEPS * (half + 1))
                act.activation(y_sb[:, cols], top_banks[2][0:1, :], ACT.Copy).then_inc(y_ready, 1)

        @block.tensor
        def _(pe):
            def pair1(i, k, j):
                if j == 0 and exists(i, k, 2):
                    pe.wait_ge(sum1_done, 2 * i + k - 1)
                pe.wait_ge(z1_ready, PAIRS1 * (2 * i + k) + j + 1)
                for a in range(2):
                    for half in range(2):
                        last = pe.matmul(ps1[k % 2][:, half, :], w1_sb[:, 2 * j + a, :],
                                         z1[:, j, a, half * HALF:(half + 1) * HALF],
                                         start=(j == 0 and a == 0), stop=False)
                last.then_inc(mm1_done, 1)

            def apart16(i, k):
                pe.wait_ge(z5_split, 2 * i + k + 1)
                for half in range(2):
                    last = pe.matmul(ps1[k % 2][:, half, :], w5_parts[:], z5_parts[:, half * HALF:(half + 1) * HALF],
                                     start=False, stop=True)
                last.then_inc(mm1_done, 1)

            def pair2(i, k, p):
                begin, end = p == PE_ORDER[0], p == PE_ORDER[-1]
                ps = ps2[k % 2]
                if begin and exists(i, k, 2):
                    pe.wait_ge(sum2_done, 2 * i + k - 1)
                if p in SPLIT:
                    n = SPLIT.index(p)
                    pe.wait_ge(low_ready, NS * (2 * i + k) + n + 1)
                    for a in range(2):
                        for w, z in ((w2_high, z2_high), (w2_low, z2_high), (w2_high, z2_low)):
                            for half in range(2):
                                last = pe.matmul(ps[:, half, :], w[:, 2 * n + a, :],
                                                 z[:, part_slot(k, n), a, half * HALF:(half + 1) * HALF],
                                                 start=(begin and a == 0 and w is w2_high and z is z2_high),
                                                 stop=(end and a == 1 and z is z2_low))
                else:
                    pe.wait_ge(z2_ready, PAIRS2 * (2 * i + k) + p + 1)
                    for a in range(2):
                        for half in range(2):
                            last = pe.matmul(ps[:, half, :], w2_sb[:, 2 * FULL.index(p) + a, :],
                                             z2[:, p % 4, a, half * HALF:(half + 1) * HALF],
                                             start=(begin and a == 0), stop=(end and a == 1))
                last.then_inc(mm2_done, 1)

            def keep_awake(n):
                for _ in range(n):
                    pe.matmul(ps2[1][:, 0, :], w2_sb[:, 0, :], w2_sb[:, 0:4, :], start=True, stop=True)

            def phase(i, k):
                pair1(i, k + 1, 0)
                pair2(i, k, PE_ORDER[0])
                pair1(i, k + 1, 1)
                apart16(i, k + 1)
                for p in PE_ORDER[1:]:
                    pair2(i, k, p)

            pe.wait_ge(w1_ready, 1)
            pe.wait_ge(w5_ready, 1)
            pe.wait_ge(w2_ready, PAIRS2)
            pe.wait_ge(stored0, 16 * STORES)
            keep_awake(8)
            pair1(0, 0, 0)
            pair1(0, 0, 1)
            apart16(0, 0)
            pair1(0, 1, 0)
            keep_awake(2)
            pair2(0, 0, PE_ORDER[0])
            pair1(0, 1, 1)
            apart16(0, 1)
            for p in PE_ORDER[1:]:
                pair2(0, 0, p)
            phase(0, 1)
            with pe.Fori(1, LOOPS) as i:
                phase(i, 0)
                phase(i, 1)
            phase(LOOPS, 0)
            for p in PE_ORDER:
                pair2(LOOPS, 1, p)

            pe.wait_ge(top_here, 112)
            for half in range(2):
                cols = slice(half * HALF, (half + 1) * HALF)
                pe.wait_ge(kept1, CH)
                pe.wait_ge(kept2, CH - 1 if half == 0 else CH)
                for m in range(4):
                    if half:
                        pe.wait_ge(y_ready, 1)
                    pe.matmul(top_banks[m], wt1a_sb[:, m * P:(m + 1) * P], feat_a[:, cols], start=True, stop=False)
                    pe.matmul(top_banks[m], wt1b_sb[:, m * P:(m + 1) * P], feat_b[:, cols], start=False,
                              stop=True).then_inc(top_mm, 1)
                pe.wait_ge(h1_ready, 4 * (half + 1))
                for m in range(2):
                    for kt in range(4):
                        last = pe.matmul(top_banks[m], wt2_sb[:, kt, m * P:(m + 1) * P], h1[:, kt, cols],
                                         start=(kt == 0), stop=(kt == 3))
                    last.then_inc(top_mm, 1)
                pe.wait_ge(h2_ready, 2 * (half + 1))
                for kt in range(2):
                    last = pe.matmul(top_banks[2][0:1, :], wt3_sb[:, kt:kt + 1], h2[:, kt, cols],
                                     start=(kt == 0), stop=(kt == 1))
                last.then_inc(top_mm, 1)


def layouts(inputs):
    a = {k: np.asarray(v) for k, v in inputs.items()}
    out = {}
    out["table"] = np.concatenate([a[f"tbl_{f}"] for f in range(F0)])
    out["ids"] = np.ascontiguousarray(a["ids"].reshape(2, 2, B // 4, F0).transpose(0, 3, 1, 2).reshape(P, B // 4))
    out["ids"] = np.concatenate([out["ids"], np.zeros((P, JG), out["ids"].dtype)], axis=1)
    first = np.concatenate([[0], np.cumsum(ROWS)[:-1]]).astype(np.int32)
    base = np.broadcast_to(first[None, :, None, None], (2, F0, 2, B // 4 + JG))
    out["base"] = np.ascontiguousarray(base.reshape(P, -1))
    out["dense"] = np.ascontiguousarray(
        a["dense_ctx"].reshape(2, 2, GROUPS, JG, DENSE).transpose(4, 2, 0, 1, 3).reshape(DENSE, B))
    w1 = a["L0_rec_W1"].reshape(O, F0, F0)
    t, i, k = np.ix_(np.arange(4), np.arange(F0), np.arange(REPS))
    one, other = i + 0 * t + 0 * k, (i + 4 * t + k) % F0
    tile = lambda x: np.ascontiguousarray(x.transpose(2, 3, 1, 0).reshape(P, -1, O))
    there, back = w1[:, one, other], w1[:, other, one].copy()
    back[:, 0, :, 0] = 0
    out["w1a"], out["w1b"] = tile(there), tile(back)
    i = np.arange(APART)
    orders = np.stack([w1[:, i, i + APART]] * 2 + [w1[:, i + APART, i]] * 2, axis=-1)
    out["w1c"] = np.ascontiguousarray(np.concatenate([orders.transpose(1, 2, 0).reshape(64, O)] * 2))
    out["w5_minus"] = np.tile(np.array([0, -1], np.float32), P // 2).reshape(P, 1)
    w2 = a["L0_rec_W2"].reshape(O, HID, F0)
    p, u, i, k = np.ix_(np.arange(PAIRS2), np.arange(2), np.arange(F0), np.arange(REPS))
    row = 32 * u + (i + APART * np.array(ARR)[p]) % F0 + 0 * k
    field = (i + 4 * np.array(TILE)[p] + k + 0 * u) % F0
    out["w2"] = np.ascontiguousarray(w2[:, row, field].transpose(3, 4, 1, 2, 0).reshape(P, 2 * PAIRS2, O))
    out["b1"], out["b2"] = a["L0_rec_b1"].reshape(P, 1), a["L0_rec_b2"].reshape(P, 1)
    wt1 = a["W_top1"]
    out["wt1a"] = np.ascontiguousarray(wt1[HID:HID + O])
    out["wt1b"] = np.concatenate([wt1[HID + O:], np.zeros((64 - DENSE, TOP1), np.float32), wt1[:HID]])
    out["bt1"] = np.ascontiguousarray(a["b_top1"].reshape(4, P).T)
    out["wt2"] = np.ascontiguousarray(a["W_top2"].reshape(4, P, TOP2).transpose(1, 0, 2))
    out["bt2"] = np.ascontiguousarray(a["b_top2"].reshape(2, P).T)
    out["wt3"] = np.ascontiguousarray(a["W_top3"].reshape(2, P).T)
    return out


def kernel(**inputs):
    import concourse.bacc as bacc
    from concourse.bass_utils import run_bass_kernel_spmd

    nc = bacc.Bacc("TRN2", target_bir_lowering=False, num_devices=1)
    arrays = layouts(inputs)
    args = {name: nc.dram_tensor(f"in_{name}", x.shape, mybir.dt.from_np(x.dtype), kind="ExternalInput").ap()
            for name, x in arrays.items()}
    out = nc.dram_tensor("out_y", (1, B), mybir.dt.float32, kind="ExternalOutput").ap()
    build(nc, y=out, **args)
    r = run_bass_kernel_spmd(nc, [{f"in_{n}": x for n, x in arrays.items()}], core_ids=[0])
    got = r.results[0]["out_y"]
    return np.ascontiguousarray(got.reshape(GROUPS, 2, 2, JG).transpose(1, 2, 0, 3).reshape(B, 1))
```
